# Optimizing a Trainium2 kernel written in Bass

```python
import numpy as np
import jax
import jax.numpy as jnp

def _softmax(x, axis=-1):
    return jax.nn.softmax(x, axis=axis)
def _gelu(x):
    return jax.nn.gelu(x, approximate=True)
def _silu(x):
    return jax.nn.silu(x)
def _sigmoid(x):
    return jax.nn.sigmoid(x)
def _layernorm(x, axis=-1, eps=1e-5):
    m = jnp.mean(x, axis=axis, keepdims=True)
    v = jnp.var(x, axis=axis, keepdims=True)
    return (x - m) / jnp.sqrt(v + eps)
def _scatter_add(tgt, idx, src, axis=0):
    return tgt.at[idx].add(src)
def _segment_sum(src, seg, n):
    return jax.ops.segment_sum(src, seg, n)

kernel_name = 'mk_metaformer_d1_conv_nchw128_fd0181'

def setup_inputs(seed: int = 0):
    np.random.seed(seed)
    _w = jnp.asarray
    def _rec_inputs():
        import jax
        import jax.numpy as jnp
        _gk = jax.random.key(seed)
        x = 7.22e-05 + 1 * jax.random.normal(jax.random.fold_in(_gk, 1), (4, 128, 128, 128), jnp.float32)
        return x
    x = _rec_inputs()
    def _L0_conv_setup():
        import jax, jax.numpy as jnp
        import numpy as np
        DIM = 128
        HID = 4 * DIM
        EPS = 1e-05

        def _ln(x, g, b):
            mu = jnp.mean(x, axis=-1, keepdims=True)
            var = jnp.mean(jnp.square(x - mu), axis=-1, keepdims=True)
            return (x - mu) * jax.lax.rsqrt(var + EPS) * g + b

        def _block(x, ln0_g, ln0_b, ln1_g, ln1_b, ln2_g, ln2_b, W_out, W_whiten, W_key, W_recep, W_value):
            b, c, h, w = x.shape
            t = x.reshape(b, c, h * w).transpose(0, 2, 1)
            t = _ln(t, ln0_g, ln0_b)
            y1 = _ln(t, ln1_g, ln1_b)
            att = jnp.einsum('btc,oc->bto', jax.nn.sigmoid(y1) * y1, W_out)
            t = t + att
            y2 = _ln(t, ln2_g, ln2_b)
            wht = jnp.einsum('btc,oc->bto', y2, W_whiten)
            k = jnp.square(jax.nn.relu(jnp.einsum('btc,hc->bth', wht, W_key)))
            kv = jnp.einsum('bth,ch->btc', k, W_value)
            r = jax.nn.sigmoid(jnp.einsum('btc,oc->bto', wht, W_recep))
            t = t + r * kv
            return t.transpose(0, 2, 1).reshape(b, c, h, w)
        key = jax.random.key(seed)
        ks = jax.random.split(key, 8)
        b, c, h, w = (4, DIM, 128, 128)
        inp = {'inp_img': jax.random.normal(ks[0], (b, c, h, w), dtype=jnp.float32), 'ln0_g': jnp.ones((c,), jnp.float32), 'ln0_b': jnp.zeros((c,), jnp.float32), 'ln1_g': jnp.ones((c,), jnp.float32), 'ln1_b': jnp.zeros((c,), jnp.float32), 'ln2_g': jnp.ones((c,), jnp.float32), 'ln2_b': jnp.zeros((c,), jnp.float32), 'W_out': jax.random.normal(ks[1], (c, c), jnp.float32) * 0.05, 'W_whiten': jax.random.normal(ks[2], (c, c), jnp.float32) * 0.05, 'W_key': jax.random.normal(ks[3], (HID, c), jnp.float32) * 0.05, 'W_recep': jax.random.normal(ks[4], (c, c), jnp.float32) * 0.05, 'W_value': jax.random.normal(ks[5], (c, HID), jnp.float32) * 0.05}
        return inp
    _L0_conv_all = _L0_conv_setup()
    _L0_conv_in = {k: v for k, v in _L0_conv_all.items() if k in ('ln0_g', 'ln0_b', 'ln1_g', 'ln1_b', 'ln2_g', 'ln2_b', 'W_out', 'W_whiten', 'W_key', 'W_recep', 'W_value', )}
    del _L0_conv_all

    def _L0_ffn_setup():
        import jax, jax.numpy as jnp
        import numpy as np
        B, N, D, C, E, K = (8, 8192, 128, 128, 8, 2)
        key = jax.random.key(seed)
        k0, k1, k2 = jax.random.split(key, 3)
        x = jax.random.normal(k0, (B, N, D), dtype=jnp.float32)
        router_w = jax.random.normal(k1, (D, E), dtype=jnp.float32) * 0.05
        router_b = jnp.zeros((E,), dtype=jnp.float32)
        expert_w = jax.random.normal(k2, (E, D, C), dtype=jnp.float32) * (1.0 / np.sqrt(D))
        expert_b = jnp.zeros((E, C), dtype=jnp.float32)
        return {'x': x, 'router_w': router_w, 'router_b': router_b, 'expert_w': expert_w, 'expert_b': expert_b}
    _L0_ffn_all = _L0_ffn_setup()
    _L0_ffn_in = {k: v for k, v in _L0_ffn_all.items() if k in ('router_w', 'router_b', 'expert_w', 'expert_b', )}
    del _L0_ffn_all

    return {
        "x": x,
        "L0_conv_ln0_g": _L0_conv_in["ln0_g"],
        "L0_conv_ln0_b": _L0_conv_in["ln0_b"],
        "L0_conv_ln1_g": _L0_conv_in["ln1_g"],
        "L0_conv_ln1_b": _L0_conv_in["ln1_b"],
        "L0_conv_ln2_g": _L0_conv_in["ln2_g"],
        "L0_conv_ln2_b": _L0_conv_in["ln2_b"],
        "L0_conv_W_out": _L0_conv_in["W_out"],
        "L0_conv_W_whiten": _L0_conv_in["W_whiten"],
        "L0_conv_W_key": _L0_conv_in["W_key"],
        "L0_conv_W_recep": _L0_conv_in["W_recep"],
        "L0_conv_W_value": _L0_conv_in["W_value"],
        "L0_ffn_router_w": _L0_ffn_in["router_w"],
        "L0_ffn_router_b": _L0_ffn_in["router_b"],
        "L0_ffn_expert_w": _L0_ffn_in["expert_w"],
        "L0_ffn_expert_b": _L0_ffn_in["expert_b"],
    }

def reference(x, L0_conv_ln0_g, L0_conv_ln0_b, L0_conv_ln1_g, L0_conv_ln1_b, L0_conv_ln2_g, L0_conv_ln2_b, L0_conv_W_out, L0_conv_W_whiten, L0_conv_W_key, L0_conv_W_recep, L0_conv_W_value, L0_ffn_router_w, L0_ffn_router_b, L0_ffn_expert_w, L0_ffn_expert_b):
    import jax
    import jax.numpy as jnp
    def _L0_conv_ref(inp_img, ln0_g, ln0_b, ln1_g, ln1_b, ln2_g, ln2_b, W_out, W_whiten, W_key, W_recep, W_value):
        import jax, jax.numpy as jnp
        import numpy as np
        DIM = 128
        HID = 4 * DIM
        EPS = 1e-05

        def _ln(x, g, b):
            mu = jnp.mean(x, axis=-1, keepdims=True)
            var = jnp.mean(jnp.square(x - mu), axis=-1, keepdims=True)
            return (x - mu) * jax.lax.rsqrt(var + EPS) * g + b

        def _block(x, ln0_g, ln0_b, ln1_g, ln1_b, ln2_g, ln2_b, W_out, W_whiten, W_key, W_recep, W_value):
            b, c, h, w = x.shape
            t = x.reshape(b, c, h * w).transpose(0, 2, 1)
            t = _ln(t, ln0_g, ln0_b)
            y1 = _ln(t, ln1_g, ln1_b)
            att = jnp.einsum('btc,oc->bto', jax.nn.sigmoid(y1) * y1, W_out)
            t = t + att
            y2 = _ln(t, ln2_g, ln2_b)
            wht = jnp.einsum('btc,oc->bto', y2, W_whiten)
            k = jnp.square(jax.nn.relu(jnp.einsum('btc,hc->bth', wht, W_key)))
            kv = jnp.einsum('bth,ch->btc', k, W_value)
            r = jax.nn.sigmoid(jnp.einsum('btc,oc->bto', wht, W_recep))
            t = t + r * kv
            return t.transpose(0, 2, 1).reshape(b, c, h, w)
        params = (ln0_g, ln0_b, ln1_g, ln1_b, ln2_g, ln2_b, W_out, W_whiten, W_key, W_recep, W_value)
        out1 = _block(inp_img, *params)
        out2 = _block(inp_img.transpose(0, 1, 3, 2), *params).transpose(0, 1, 3, 2)
        return out2 + out1

    def _L0_ffn_ref(x, router_w, router_b, expert_w, expert_b):
        import jax, jax.numpy as jnp
        import numpy as np
        B, N, D, C, E, K = (8, 8192, 128, 128, 8, 2)
        router_probs = jax.nn.softmax(x @ router_w + router_b, axis=-1)
        top_p, top_i = jax.lax.top_k(router_probs, K)
        top_p = top_p / jnp.sum(top_p, axis=-1, keepdims=True)
        expert_out = jnp.einsum('bnd,edc->bnec', x, expert_w) + expert_b
        gathered = jnp.take_along_axis(expert_out, top_i[..., None], axis=2)
        return jnp.einsum('bnk,bnkc->bnc', top_p, gathered)

    def _gn(v, G=32, eps=1e-5):
        B_, C_, H_, W_ = v.shape
        g = v.reshape(B_, G, C_ // G, H_, W_)
        m = jnp.mean(g, axis=(2, 3, 4), keepdims=True)
        s = jnp.var(g, axis=(2, 3, 4), keepdims=True)
        return ((g - m) / jnp.sqrt(s + eps)).reshape(v.shape)

    def _ln_c(v, eps=1e-6):
        m = jnp.mean(v, axis=1, keepdims=True)
        s = jnp.var(v, axis=1, keepdims=True)
        return (v - m) / jnp.sqrt(s + eps)

    def _ln_t(v, eps=1e-5):
        m = jnp.mean(v, axis=-1, keepdims=True)
        s = jnp.var(v, axis=-1, keepdims=True)
        return (v - m) / jnp.sqrt(s + eps)

    def _to_tokens(v):
        B_, C_, H_, W_ = v.shape
        return v.reshape(B_, C_, H_ * W_).transpose(0, 2, 1)
    def _from_tokens(t, like):
        B_, C_, H_, W_ = like.shape
        return t.transpose(0, 2, 1).reshape(B_, C_, H_, W_)

    x = x + _L0_conv_ref(_ln_c(x), L0_conv_ln0_g, L0_conv_ln0_b, L0_conv_ln1_g, L0_conv_ln1_b, L0_conv_ln2_g, L0_conv_ln2_b, L0_conv_W_out, L0_conv_W_whiten, L0_conv_W_key, L0_conv_W_recep, L0_conv_W_value)
    t = _to_tokens(x)
    t = t + _L0_ffn_ref(_ln_t(t), L0_ffn_router_w, L0_ffn_router_b, L0_ffn_expert_w, L0_ffn_expert_b)
    x = _from_tokens(t, x)
    return x


_drawn_inputs = setup_inputs


def setup_inputs(seed=0):
    import zlib

    import numpy as np

    out = dict(_drawn_inputs(seed))
    spreads = {'L0_conv_ln0_g': (1.0, 0.2),
     'L0_conv_ln0_b': (0.0, 0.1),
     'L0_conv_ln1_g': (1.0, 0.2),
     'L0_conv_ln1_b': (0.0, 0.1),
     'L0_conv_ln2_g': (1.0, 0.598),
     'L0_conv_ln2_b': (0.0, 0.449),
     'L0_ffn_router_b': (0.0, 0.1),
     'L0_ffn_expert_b': (0.0, 0.36)}
    factors = {'L0_conv_W_recep': 3.133}
    for name, (base, spread) in spreads.items():
        noise = np.random.default_rng([zlib.crc32(name.encode()), seed]).standard_normal(out[name].shape)
        drawn = base * np.exp(spread * noise) if base else spread * noise
        out[name] = jnp.asarray(drawn.astype(out[name].dtype))
    for name, factor in factors.items():
        out[name] = (out[name] * factor).astype(out[name].dtype)
    return out
```

```python
from contextlib import ExitStack

import concourse.bass as bass
from concourse import mybir

P = 128
TILES = 4
TOKENS = TILES * P
SLOTS = 2
ACT = mybir.ActivationFunctionType
ALU = mybir.AluOpType
F32 = mybir.dt.float32
F32R = mybir.dt.float32r
U32 = mybir.dt.uint32

EPS_CHANNEL = 1e-6
EPS = 1e-5
DEPTH = 5
FIRST_LOOPED = 6


def metaformer_layer(
    nc: bass.Bass,
    x: bass.AP,
    ln0_g: bass.AP,
    ln0_b: bass.AP,
    ln1_g: bass.AP,
    ln1_b: bass.AP,
    ln2_g: bass.AP,
    ln2_b: bass.AP,
    w_out_t: bass.AP,
    w_whiten: bass.AP,
    w_key_t: bass.AP,
    w_recep_t: bass.AP,
    w_value_t: bass.AP,
    router_w: bass.AP,
    router_b: bass.AP,
    expert_w: bass.AP,
    expert_b: bass.AP,
    identity: bass.AP,
    out: bass.AP,
):
    B, C, H, W = x.shape
    HID = w_key_t.shape[1]
    HB = HID // P
    E = router_w.shape[1]
    HALF = E // 2
    PER_IMAGE = H * W // TOKENS
    GROUPS = B * PER_IMAGE
    CHUNKS = 2 * TILES
    assert C == P and H * W % TOKENS == 0 and HALF * P == TOKENS and HB == 4 and E == 8
    last_looped = GROUPS - (GROUPS - FIRST_LOOPED) % 2

    x_groups = x.rearrange("b c h w -> b c (h w)").rearrange("b c (n t) -> c b n t", t=TOKENS)
    out_groups = out.rearrange("b c h w -> b c (h w)").rearrange("b c (n t) -> c b n t", t=TOKENS)

    with ExitStack() as ctx:
        def sb(name, shape, dt=F32):
            return ctx.enter_context(nc.sbuf_tensor(name, shape, dt))

        def sem(name):
            return ctx.enter_context(nc.semaphore(name))

        bank = [ctx.enter_context(nc.psum_tensor(f"bank{i}", [P, TOKENS], F32)) for i in range(8)]
        turn_a, turn_b, token_sum = bank[0], bank[1], bank[2]
        hidden = [bank[3], bank[4], bank[3], bank[4]]
        expert_ring = [bank[5], bank[6], bank[7], bank[2]]

        def tiled(t):
            return t[:].rearrange("p (t c) -> p t c", t=TILES)

        ident = sb("ident", [P, P])
        over_c = sb("over_c", [P, P])
        less_over_c = sb("less_over_c", [P, P])
        minus_half = sb("minus_half", [P, TILES])
        expert_ids = sb("expert_ids", [P, 2, E])
        g0_row = sb("g0_row", [P, C])
        b0_row = sb("b0_row", [P, C])
        cols = sb("cols", [P, 5])
        g1_col, b1_col, g2_col, b2_col, b2_less_g2 = (cols[:, i:i + 1] for i in range(5))
        wout = sb("wout", [P, C])
        wvalue = sb("wvalue", [P, HB, C])
        mix_hi = sb("mix_hi", [P, HID + C], F32R)
        mix_lo = sb("mix_lo", [P, HID + C], F32R)
        exp_hi = sb("exp_hi", [P, E * C], F32R)
        exp_lo = sb("exp_lo", [P, E * C], F32R)
        rout_hi = sb("rout_hi", [P, E], F32R)
        rout_lo = sb("rout_lo", [P, E], F32R)
        whiten = sb("whiten", [P, C])
        keyrecep = sb("keyrecep", [P, HID + C])
        raw_exp = sb("raw_exp", [P, E * C])
        raw_rout = sb("raw_rout", [P, E])
        exp_bias = sb("exp_bias", [1, E * C])
        rout_bias = sb("rout_bias", [1, E])
        merged = sb("merged", [P, HID + C])
        scaled = sb("scaled", [P, HID + C])
        full = sb("full", [P, E * C])
        full_rout = sb("full_rout", [P, E])

        x_in = sb("x_in", [P, SLOTS, TOKENS])
        x_tok = sb("x_tok", [P, SLOTS, TILES, C])
        bn = sb("bn", [P, 4, TILES, 6])
        gap = sb("gap", [P, 4, TILES])
        gap_square = sb("gap_square", [P, 4, TILES])
        both = sb("both", [P, 4, TILES, 2])
        moment = sb("moment", [P, 4, TILES])
        var_eps = sb("var_eps", [P, 4, TILES])
        neg_mean = sb("neg_mean", [P, 4, TILES])
        rstd = sb("rstd", [P, 4, TILES])
        shift = sb("shift", [P, 4, TILES])
        centred = sb("centred", [P, TILES, C])
        t0 = sb("t0", [P, TILES, C])
        z1 = sb("z1", [P, TILES, C])
        silu = sb("silu", [P, TOKENS])
        t1 = sb("t1", [P, TILES, C])
        carried = sb("carried", [P, SLOTS, TILES, C])
        z2 = sb("z2", [P, TILES, C])
        z2_hi = sb("z2_hi", [P, TOKENS], F32R)
        z2_lo = sb("z2_lo", [P, TOKENS], F32R)
        relu = sb("relu", [P, 2, TOKENS])
        squared = sb("squared", [P, HB, TOKENS])
        gate_tanh = sb("gate_tanh", [P, TILES, C])
        gated_kv = sb("gated_kv", [P, TILES, C])
        x1 = sb("x1", [P, SLOTS, TILES, C])
        z3 = sb("z3", [P, TILES, C])
        z3_hi = sb("z3_hi", [P, TOKENS], F32R)
        z3_lo = sb("z3_lo", [P, TOKENS], F32R)
        top_logit = sb("top_logit", [P, TILES, 8])
        top_index = sb("top_index", [P, TILES, 8], U32)
        top_id = sb("top_id", [P, TILES, 2])
        logit_gap = sb("logit_gap", [P, TILES])
        gap_tanh = sb("gap_tanh", [P, TILES])
        top_prob = sb("top_prob", [P, TILES, 2])
        one_hot = sb("one_hot", [P, TILES, 2, E])
        gates = sb("gates", [P, TILES, E])
        weighted = sb("weighted", [P, 4, HALF * C])
        half_sum = sb("half_sum", [P, 2, HALF * C])
        quarter_sum = sb("quarter_sum", [P, TILES, 2, C])
        y_out = sb("y_out", [P, SLOTS, TOKENS])

        weights_loaded, prep_pe, prep_dve, prep_pool = (sem(n) for n in ("weights_loaded", "prep_pe", "prep_dve", "prep_pool"))
        x_loaded = [sem(f"x_loaded{i}") for i in range(SLOTS)]
        y_stored = [sem(f"y_stored{i}") for i in range(SLOTS)]
        x_turned, z1_turned, z2_turned, z3_turned = (sem(n) for n in ("x_turned", "z1_turned", "z2_turned", "z3_turned"))
        att_done, recep_done, value_done, router_done, y_turned = (
            sem(n) for n in ("att_done", "recep_done", "value_done", "router_done", "y_turned"))
        key_done = sem("key_done")
        experts_done = sem("experts_done")
        x_tok_ready, z1_ready, silu_ready, z2_ready, z2_hi_ready = (
            sem(n) for n in ("x_tok_ready", "z1_ready", "silu_ready", "z2_ready", "z2_hi_ready"))
        relu_ready, squared_ready = sem("relu_ready"), sem("squared_ready")
        gate_ready, z3_ready, z3_hi_ready, gap_tanh_ready, y_ready = (
            sem(n) for n in ("gate_ready", "z3_ready", "z3_hi_ready", "gap_tanh_ready", "y_ready"))
        bn_ready, gap_ready, both_ready, gap_square_ready, moment_ready, neg_mean_ready, var_eps_ready = (
            [sem(f"{n}{i}_ready") for i in range(4)] for n in ("bn", "gap", "both", "gap_square", "moment", "neg_mean", "var_eps"))
        centred_ready, t0_ready, t1_ready, carried_ready, z2_lo_ready = (
            sem(n) for n in ("centred_ready", "t0_ready", "t1_ready", "carried_ready", "z2_lo_ready"))
        gated_kv_ready, x1_ready, z3_lo_ready = (sem(n) for n in ("gated_kv_ready", "x1_ready", "z3_lo_ready"))
        top_logit_ready, top_index_ready, logit_gap_ready, top_id_ready, top_prob_ready, one_hot_ready, one_hot_weighted, gates_ready = (
            sem(n) for n in ("top_logit_ready", "top_index_ready", "logit_gap_ready", "top_id_ready", "top_prob_ready",
                             "one_hot_ready", "one_hot_weighted", "gates_ready"))
        weighted_ready = sem("weighted_ready")
        rstd_ready, shift_ready = ([sem(f"{n}{i}_ready") for i in range(4)] for n in ("rstd", "shift"))
        half_sum_ready, quarter_sum_ready = sem("half_sum_ready"), sem("quarter_sum_ready")

        def count(g, per=1, extra=0):
            return (g + 1) * per + extra

        def live(g):
            return 0 <= g < GROUPS if isinstance(g, int) else True

        def wait_for(eng, semaphore, g, per=1, extra=0):
            if live(g):
                eng.wait_ge(semaphore, count(g, per, extra))

        def wait_first(eng, *choices):
            for semaphore, g, per, extra in choices:
                if live(g):
                    eng.wait_ge(semaphore, count(g, per, extra))
                    return

        def run_steps(eng, step):
            for s in range(FIRST_LOOPED):
                step(s, s % 2)
            with eng.Fori(FIRST_LOOPED // 2, last_looped // 2) as pair:
                for k in range(2):
                    step(pair * 2 + k, k)
            for s in range(last_looped, GROUPS + DEPTH):
                step(s, s % 2)

        block = ctx.enter_context(nc.Block())

        @block.sync
        def _(sp):
            loads = [
                (ident[:], identity), (whiten[:], w_whiten), (keyrecep[:, 0:HID], w_key_t), (keyrecep[:, HID:], w_recep_t),
                (cols[:, 0:1], ln1_g.unsqueeze(1)), (cols[:, 1:2], ln1_b.unsqueeze(1)),
                (cols[:, 2:3], ln2_g.unsqueeze(1)), (cols[:, 3:4], ln2_b.unsqueeze(1)),
                (g0_row[:], ln0_g.unsqueeze(0).to_broadcast([P, C])), (b0_row[:], ln0_b.unsqueeze(0).to_broadcast([P, C])),
                (raw_exp[:].rearrange("p (e c) -> p e c", e=E), expert_w.rearrange("e d c -> d e c")),
                (raw_rout[:], router_w), (exp_bias[:], expert_b.rearrange("e c -> (e c)").unsqueeze(0)),
                (rout_bias[:], router_b.unsqueeze(0)), (wout[:], w_out_t),
                (wvalue[:], w_value_t.rearrange("(j p) c -> p j c", p=P)),
            ]
            assert len(loads) == N_LOADS
            for g in range(2):
                sp.dma_start(x_in[:, g, :], x_groups[:, 0, g, :]).then_inc(x_loaded[g], 16)
            for dst, src in loads:
                sp.dma_start(dst, src).then_inc(weights_loaded, 16)

            def step(s, k):
                g = s - 5
                if live(g):
                    wait_for(sp, y_ready, g)
                    sp.dma_start(out_groups[:, g // PER_IMAGE, g % PER_IMAGE, :], y_out[:, 1 - k, :]).then_inc(y_stored[1 - k], 16)
                g = s + 2
                if live(g):
                    wait_for(sp, x_turned, s)
                    sp.dma_start(x_in[:, k, :], x_groups[:, g // PER_IMAGE, g % PER_IMAGE, :]).then_inc(x_loaded[k], 16)

            for s in range(FIRST_LOOPED):
                step(s, s % 2)
            with sp.Fori(FIRST_LOOPED // 2, last_looped // 2 - 1) as pair:
                for k in range(2):
                    step(pair * 2 + k, k)
            for s in range(last_looped - 2, GROUPS + DEPTH):
                step(s, s % 2)
            for k in range(SLOTS):
                sp.wait_ge(y_stored[k], 16 * ((GROUPS + 1 - k) // 2))

        @block.tensor
        def _(pe):
            def split_product(dst, lhs_hi, lhs_lo, rhs_hi, rhs_lo):
                pe.matmul(dst, lhs_hi, rhs_hi, start=True, stop=False)
                pe.matmul(dst, lhs_hi, rhs_lo, start=False, stop=False)
                return pe.matmul(dst, lhs_lo, rhs_hi, start=False, stop=True)

            pe.wait_ge(weights_loaded, 16 * N_LOADS)
            pe.wait_ge(prep_pool, 1)
            pe.matmul(bank[3][:], whiten[:], keyrecep[:, 0:HID], start=True, stop=True)
            pe.matmul(bank[4][:, 0:C], whiten[:], keyrecep[:, HID:], start=True, stop=True).then_inc(prep_pe, 1)
            pe.wait_ge(prep_dve, 3)
            pe.matmul(bank[5][:], over_c[:], scaled[:, 0:HID], start=True, stop=True)
            pe.matmul(bank[6][:, 0:C], over_c[:], scaled[:, HID:], start=True, stop=True).then_inc(prep_pe, 1)
            for h in range(2):
                part = slice(h * TOKENS, (h + 1) * TOKENS)
                pe.matmul(bank[1 + h][:], less_over_c[:], raw_exp[:, part], start=True, stop=False)
                pe.matmul(bank[1 + h][:], over_c[0:1, :], exp_bias[:, part], start=False, stop=True)
            pe.matmul(bank[7][:, 0:E], less_over_c[:], raw_rout[:], start=True, stop=False)
            pe.matmul(bank[7][:, 0:E], over_c[0:1, :], rout_bias[:], start=False, stop=True).then_inc(prep_pe, 1)
            pe.wait_ge(prep_dve, 9)

            def turn(dst, src_tile, done):
                for t in range(TILES):
                    last = pe.transpose(dst[:, t * P:(t + 1) * P], src_tile(t), ident[:])
                last.then_inc(done, 1)

            def step(s, k):
                g = s - 2
                if live(g):
                    wait_for(pe, z2_ready, g)
                    wait_for(pe, z3_lo_ready, s - 4)
                    turn(turn_a, lambda t: z2[:, t, :], z2_turned)
                g = s
                if live(g):
                    pe.wait_ge(x_loaded[k], load_count(g, k))
                    wait_for(pe, silu_ready, s - 1)
                    turn(turn_b, lambda t: x_in[:, k, t * P:(t + 1) * P], x_turned)
                g = s - 1
                if live(g):
                    wait_for(pe, silu_ready, g)
                    wait_for(pe, weighted_ready, s - 5, CHUNKS)
                    for t in range(TILES):
                        last = pe.matmul(token_sum[:, t * C:(t + 1) * C], silu[:, t * P:(t + 1) * P], wout[:], start=True, stop=True)
                    last.then_inc(att_done, 1)
                g = s - 5
                if live(g):
                    wait_for(pe, quarter_sum_ready, g, TILES)
                    wait_first(pe, (z2_lo_ready, s - 2, 1, 0), (z3_lo_ready, s - 4, 1, 0))
                    for t in range(TILES):
                        dst = turn_a[:, t * P:(t + 1) * P]
                        pe.matmul(dst, x1[:, 1 - k, t, :], ident[:], is_transpose=True, start=True, stop=False)
                        pe.matmul(dst, quarter_sum[:, t, 0, :], ident[:], is_transpose=True, start=False, stop=False)
                        last = pe.matmul(dst, quarter_sum[:, t, 1, :], ident[:], is_transpose=True, start=False, stop=True)
                    last.then_inc(y_turned, 1)
                g = s - 4
                if live(g):
                    wait_for(pe, z3_lo_ready, g)
                    wait_first(pe, (x_tok_ready, s, 1, 0), (silu_ready, s - 1, 1, 0))
                    for t in range(TILES):
                        tok = slice(t * P, (t + 1) * P)
                        last = split_product(turn_b[:, t * E:(t + 1) * E], z3_hi[:, tok], z3_lo[:, tok], rout_hi[:], rout_lo[:])
                    last.then_inc(router_done, 1)
                g = s - 3
                if live(g):
                    wait_for(pe, squared_ready, g, HB)
                    wait_first(pe, (t1_ready, s - 1, 1, 0), (weighted_ready, s - 5, CHUNKS, 0))
                    for t in range(TILES):
                        for j in range(HB):
                            last = pe.matmul(token_sum[:, t * C:(t + 1) * C], squared[:, j, t * P:(t + 1) * P], wvalue[:, j, :],
                                             start=(j == 0), stop=(j == HB - 1))
                    last.then_inc(value_done, 1)
                g = s - 2
                if live(g):
                    wait_for(pe, z2_lo_ready, g)
                    for j in range(HB):
                        if j < 2:
                            wait_for(pe, relu_ready, g - 1, HB)
                        else:
                            eng_wait = count(g - 1, HB, j - 1)
                            pe.wait_ge(relu_ready, eng_wait)
                        cut = slice(j * P, (j + 1) * P)
                        split_product(hidden[j][:], mix_hi[:, cut], mix_lo[:, cut], z2_hi[:], z2_lo[:]).then_inc(key_done, 1)
                    wait_for(pe, y_ready, s - 5)
                    for t in range(TILES):
                        tok = slice(t * P, (t + 1) * P)
                        last = split_product(turn_a[:, t * C:(t + 1) * C], z2_hi[:, tok], z2_lo[:, tok], mix_hi[:, HID:], mix_lo[:, HID:])
                    last.then_inc(recep_done, 1)
                g = s - 4
                if live(g):
                    for c in range(CHUNKS):
                        t, h = divmod(c, 2)
                        if c == 3:
                            wait_first(pe, (gated_kv_ready, s - 3, 1, 0), (weighted_ready, g - 1, CHUNKS, 0))
                        elif c < 3:
                            wait_for(pe, weighted_ready, g - 1, CHUNKS)
                        else:
                            pe.wait_ge(weighted_ready, count(g - 1, CHUNKS, c - 3))
                        tok, cut = slice(t * P, (t + 1) * P), slice(h * TOKENS, (h + 1) * TOKENS)
                        split_product(expert_ring[c % 4][:], z3_hi[:, tok], z3_lo[:, tok], exp_hi[:, cut], exp_lo[:, cut]
                                      ).then_inc(experts_done, 1)
                g = s - 3
                if live(g):
                    wait_for(pe, z3_ready, g)
                    wait_first(pe, (gate_ready, s - 2, 1, 0), (y_ready, s - 5, 1, 0))
                    turn(turn_a, lambda t: z3[:, t, :], z3_turned)
                g = s
                if live(g):
                    wait_for(pe, z1_ready, g)
                    wait_for(pe, top_index_ready, s - 4)
                    turn(turn_b, lambda t: z1[:, t, :], z1_turned)

            run_steps(pe, step)

        @block.scalar
        def _(act):
            def normalise(dst, src, ln, g, ready):
                wait_for(act, shift_ready[ln], g)
                for t in range(TILES):
                    last = act.activation(dst[:, t, :], src[:, t, :], ACT.Identity,
                                          bias=shift[:, ln, t:t + 1], scale=rstd[:, ln, t:t + 1])
                last.then_inc(ready, 1)

            act.wait_ge(weights_loaded, 16 * N_LOADS)

            def step(s, k):
                g = s - 2
                if live(g):
                    wait_for(act, z2_turned, g)
                    wait_for(act, recep_done, g - 1)
                    act.activation(z2_hi[:], turn_a[:], ACT.Identity, bias=1.0).then_inc(z2_hi_ready, 1)
                g = s
                if live(g):
                    wait_for(act, x_turned, g)
                    wait_for(act, carried_ready, g - 2)
                    act.activation(x_tok[:, k, :, :], tiled(turn_b), ACT.Copy).then_inc(x_tok_ready, 1)
                g = s - 5
                if live(g):
                    wait_for(act, y_turned, g)
                    if live(g - 2):
                        act.wait_ge(y_stored[1 - k], load_count(g - 2, 1 - k))
                    act.activation(y_out[:, 1 - k, :], turn_a[:], ACT.Copy).then_inc(y_ready, 1)
                g = s - 4
                if live(g):
                    wait_for(act, logit_gap_ready, g)
                    act.activation(gap_tanh[:], logit_gap[:], ACT.Tanh, scale=0.5).then_inc(gap_tanh_ready, 1)
                g = s - 1
                if live(g):
                    wait_for(act, z2_turned, g - 1)
                    normalise(z2, t1, 2, g, z2_ready)
                g = s - 2
                if live(g):
                    for j in range(HB):
                        act.wait_ge(key_done, count(g - 1, HB, j + 1))
                        act.activation(relu[:, j % 2, :], hidden[j][:], ACT.Relu).then_inc(relu_ready, 1)
                        if j == 0:
                            wait_for(act, value_done, g - 1)
                        act.wait_ge(relu_ready, count(g - 1, HB, j + 1))
                        act.activation(squared[:, j, :], relu[:, j % 2, :], ACT.Square).then_inc(squared_ready, 1)
                    wait_for(act, recep_done, g)
                    wait_for(act, gated_kv_ready, g - 1)
                    act.activation(gate_tanh[:], tiled(turn_a), ACT.Tanh, scale=0.5).then_inc(gate_ready, 1)
                g = s
                if live(g):
                    wait_for(act, z1_turned, g - 1)
                    normalise(z1, t0, 1, g, z1_ready)
                g = s - 3
                if live(g):
                    wait_for(act, z3_turned, g - 1)
                    normalise(z3, x1[:, 1 - k], 3, g, z3_ready)
                    wait_for(act, z3_turned, g)
                    wait_for(act, experts_done, g - 1, CHUNKS)
                    act.activation(z3_hi[:], turn_a[:], ACT.Identity, bias=1.0).then_inc(z3_hi_ready, 1)
                g = s
                if live(g):
                    wait_for(act, z1_turned, g)
                    wait_for(act, att_done, g - 1)
                    act.activation(silu[:], turn_b[:], ACT.Silu, bias=b1_col, scale=g1_col).then_inc(silu_ready, 1)

            run_steps(act, step)

        @block.vector
        def _(dve):
            dve.wait_ge(weights_loaded, 16 * N_LOADS)
            dve.tensor_tensor(b2_less_g2, b2_col, g2_col, ALU.subtract).then_inc(prep_dve, 1)
            dve.wait_ge(prep_pe, 1)
            dve.tensor_copy(merged[:, 0:HID], bank[3][:])
            dve.tensor_copy(merged[:, HID:], bank[4][:, 0:C]).then_inc(prep_dve, 1)
            dve.wait_ge(prep_dve, 2)
            dve.tensor_scalar(scaled[:], merged[:], b2_less_g2, None, ALU.mult).then_inc(prep_dve, 1)
            dve.wait_ge(prep_pe, 2)
            dve.scalar_tensor_tensor(full[:, 0:HID], merged[:, 0:HID], g2_col, bank[5][:], ALU.mult, ALU.add)
            dve.scalar_tensor_tensor(full[:, HID:HID + C], merged[:, HID:], g2_col, bank[6][:, 0:C], ALU.mult, ALU.add
                                     ).then_inc(prep_dve, 1)
            dve.wait_ge(prep_dve, 4)
            dve.tensor_copy(mix_hi[:], full[:, 0:HID + C]).then_inc(prep_dve, 1)
            dve.wait_ge(prep_dve, 5)
            dve.tensor_tensor(mix_lo[:], full[:, 0:HID + C], mix_hi[:].bitcast(F32), ALU.subtract).then_inc(prep_dve, 1)
            dve.wait_ge(prep_pe, 3)
            dve.wait_ge(prep_dve, 6)
            for h in range(2):
                part = slice(h * TOKENS, (h + 1) * TOKENS)
                dve.tensor_tensor(full[:, part], bank[1 + h][:], raw_exp[:, part], ALU.add)
            dve.tensor_tensor(full_rout[:], bank[7][:, 0:E], raw_rout[:], ALU.add).then_inc(prep_dve, 1)
            dve.wait_ge(prep_dve, 7)
            dve.tensor_copy(exp_hi[:], full[:])
            dve.tensor_copy(rout_hi[:], full_rout[:]).then_inc(prep_dve, 1)
            dve.wait_ge(prep_dve, 8)
            dve.tensor_tensor(exp_lo[:], full[:], exp_hi[:].bitcast(F32), ALU.subtract)
            dve.tensor_tensor(rout_lo[:], full_rout[:], rout_hi[:].bitcast(F32), ALU.subtract).then_inc(prep_dve, 1)
            dve.wait_ge(prep_pool, 2)

            def statistics(src, ln, g, factor=1.0, eps=EPS):
                for t in range(TILES):
                    last = dve.bn_stats(bn[:, ln, t, :], src[:, t, :])
                last.then_inc(bn_ready[ln], 1)
                dve.wait_ge(bn_ready[ln], count(g))
                dve.tensor_tensor(gap[:, ln, :], bn[:, ln, :, 1], bn[:, ln, :, 4], ALU.subtract).then_inc(gap_ready[ln], 1)
                dve.tensor_tensor(both[:, ln, :, :], bn[:, ln, :, 1:3], bn[:, ln, :, 4:6], ALU.add).then_inc(both_ready[ln], 1)
                dve.wait_ge(gap_ready[ln], count(g))
                dve.tensor_tensor(gap_square[:, ln, :], gap[:, ln, :], gap[:, ln, :], ALU.mult).then_inc(gap_square_ready[ln], 1)
                dve.wait_ge(both_ready[ln], count(g))
                wait_for(dve, shift_ready[ln] if ln else rstd_ready[ln], g - 1)
                dve.tensor_scalar(neg_mean[:, ln, :], both[:, ln, :, 0], -0.5, None, ALU.mult).then_inc(neg_mean_ready[ln], 1)
                dve.wait_ge(gap_square_ready[ln], count(g))
                dve.scalar_tensor_tensor(moment[:, ln, :], gap_square[:, ln, :], C / 4.0, both[:, ln, :, 1], ALU.mult, ALU.add
                                         ).then_inc(moment_ready[ln], 1)
                dve.wait_ge(moment_ready[ln], count(g))
                dve.tensor_scalar(var_eps[:, ln, :], moment[:, ln, :], factor / C, eps, ALU.mult, ALU.add
                                  ).then_inc(var_eps_ready[ln], 1)

            def step(s, k):
                g = s - 2
                if live(g):
                    wait_for(dve, z2_hi_ready, g)
                    wait_for(dve, recep_done, g - 1)
                    dve.scalar_tensor_tensor(z2_lo[:], turn_a[:], 1.0, z2_hi[:].bitcast(F32), ALU.add, ALU.subtract
                                             ).then_inc(z2_lo_ready, 1)
                g = s
                if live(g):
                    wait_for(dve, x_tok_ready, g)
                    statistics(x_tok[:, k], 0, g, 1.0 + EPS, EPS * EPS_CHANNEL)
                g = s - 1
                if live(g):
                    wait_for(dve, att_done, g)
                    wait_for(dve, z2_ready, g - 1)
                    dve.tensor_tensor(t1[:], tiled(token_sum), t0[:], ALU.add).then_inc(t1_ready, 1)
                    dve.wait_ge(t1_ready, count(g))
                    statistics(t1, 2, g)
                g = s
                if live(g):
                    dve.wait_ge(neg_mean_ready[0], count(g))
                    wait_for(dve, router_done, s - 4)
                    for t in range(TILES):
                        last = dve.scalar_tensor_tensor(centred[:, t, :], x_tok[:, k, t, :], neg_mean[:, 0, t:t + 1], g0_row[:],
                                                        ALU.add, ALU.mult)
                    last.then_inc(centred_ready, 1)
                g = s - 4
                if live(g):
                    if not live(s):
                        wait_for(dve, router_done, g)
                    for t in range(TILES):
                        last = dve.max(top_logit[:, t, :], turn_b[:, t * E:(t + 1) * E])
                    last.then_inc(top_logit_ready, 1)
                    dve.wait_ge(top_logit_ready, count(g))
                    wait_for(dve, gap_tanh_ready, g - 1)
                    dve.tensor_tensor(logit_gap[:], top_logit[:, :, 1], top_logit[:, :, 0], ALU.subtract).then_inc(logit_gap_ready, 1)
                    for t in range(TILES):
                        last = dve.max_index(top_index[:, t, :], top_logit[:, t, :], turn_b[:, t * E:(t + 1) * E])
                    last.then_inc(top_index_ready, 1)
                    dve.wait_ge(top_index_ready, count(g))
                    dve.tensor_copy(top_id[:], top_index[:, :, 0:2]).then_inc(top_id_ready, 1)
                    wait_for(dve, gap_tanh_ready, g)
                    dve.tensor_scalar(top_prob[:, :, 0], gap_tanh[:], -0.5, 0.5, ALU.mult, ALU.add)
                    dve.tensor_scalar(top_prob[:, :, 1], gap_tanh[:], 0.5, 0.5, ALU.mult, ALU.add).then_inc(top_prob_ready, 1)
                    dve.wait_ge(top_id_ready, count(g))
                    for j in range(2):
                        last = dve.tensor_tensor(one_hot[:, :, j, :], expert_ids[:, 0:1, :].to_broadcast([P, TILES, E]),
                                                 top_id[:, :, j:j + 1].to_broadcast([P, TILES, E]), ALU.is_equal)
                    last.then_inc(one_hot_ready, 1)
                    dve.wait_ge(top_prob_ready, count(g))
                    dve.wait_ge(one_hot_ready, count(g))
                    dve.tensor_tensor(one_hot[:], one_hot[:], top_prob[:].unsqueeze(3).to_broadcast([P, TILES, 2, E]), ALU.mult
                                      ).then_inc(one_hot_weighted, 1)
                    dve.wait_ge(one_hot_weighted, count(g))
                    dve.tensor_tensor(gates[:], one_hot[:, :, 0, :], one_hot[:, :, 1, :], ALU.add).then_inc(gates_ready, 1)
                g = s
                if live(g):
                    dve.wait_ge(centred_ready, count(g))
                    wait_for(dve, rstd_ready[0], g)
                    wait_for(dve, z1_ready, g - 1)
                    for t in range(TILES):
                        last = dve.scalar_tensor_tensor(t0[:, t, :], centred[:, t, :], rstd[:, 0, t:t + 1], b0_row[:],
                                                        ALU.mult, ALU.add)
                    last.then_inc(t0_ready, 1)
                    dve.wait_ge(t0_ready, count(g))
                    statistics(t0, 1, g)
                g = s - 3
                if live(g):
                    wait_for(dve, value_done, g)
                    wait_for(dve, gate_ready, g)
                    dve.scalar_tensor_tensor(gated_kv[:], gate_tanh[:], 1.0, tiled(token_sum), ALU.add, ALU.mult
                                             ).then_inc(gated_kv_ready, 1)
                    dve.wait_ge(gated_kv_ready, count(g))
                    dve.wait_ge(carried_ready, count(g))
                    wait_for(dve, y_turned, g - 2)
                    dve.tensor_tensor(x1[:, 1 - k], gated_kv[:], carried[:, 1 - k], ALU.add).then_inc(x1_ready, 1)
                    dve.wait_ge(x1_ready, count(g))
                    statistics(x1[:, 1 - k], 3, g)
                g = s - 1
                if live(g):
                    dve.scalar_tensor_tensor(carried[:, 1 - k], t1[:], 2.0, x_tok[:, 1 - k], ALU.mult, ALU.add
                                             ).then_inc(carried_ready, 1)
                g = s - 4
                if live(g):
                    dve.wait_ge(gates_ready, count(g))
                    for c in range(CHUNKS):
                        t, h = divmod(c, 2)
                        if c >= 4:
                            dve.wait_ge(half_sum_ready, count(g - 1, TILES, c // 2 - 1))
                        elif c % 2 == 0:
                            wait_for(dve, half_sum_ready, g - 1, TILES, c // 2 - 1)
                        dve.wait_ge(experts_done, count(g - 1, CHUNKS, c + 1))
                        dve.tensor_tensor(weighted[:, c % 4].rearrange("p (e c) -> p e c", e=HALF), tiled(expert_ring[c % 4]),
                                          gates[:, t, h * HALF:(h + 1) * HALF].unsqueeze(2).to_broadcast([P, HALF, C]), ALU.mult
                                          ).then_inc(weighted_ready, 1)
                g = s - 3
                if live(g):
                    wait_for(dve, z3_hi_ready, g)
                    dve.scalar_tensor_tensor(z3_lo[:], turn_a[:], 1.0, z3_hi[:].bitcast(F32), ALU.add, ALU.subtract
                                             ).then_inc(z3_lo_ready, 1)

            run_steps(dve, step)

        @block.gpsimd
        def _(pool):
            pool.memset(over_c[:], 1.0 / C)
            pool.memset(less_over_c[:], -1.0 / C).then_inc(prep_pool, 1)
            for e in range(E):
                pool.memset(expert_ids[:, :, e:e + 1], float(e))
            pool.memset(minus_half[:], -0.5).then_inc(prep_pool, 1)
            pool.wait_ge(prep_pool, 2)

            def inverse_std(ln, g):
                pool.wait_ge(var_eps_ready[ln], count(g))
                if ln == 0:
                    wait_for(pool, t0_ready, g - 1)
                elif ln == 1:
                    wait_for(pool, z1_ready, g - 1)
                elif ln == 2:
                    wait_for(pool, z2_ready, g - 1)
                else:
                    wait_for(pool, z3_ready, g - 1)
                pool.tensor_tensor(rstd[:, ln, :], var_eps[:, ln, :], minus_half[:], ALU.pow).then_inc(rstd_ready[ln], 1)
                if ln:
                    pool.wait_ge(neg_mean_ready[ln], count(g))
                    pool.wait_ge(rstd_ready[ln], count(g))
                    pool.tensor_tensor(shift[:, ln, :], neg_mean[:, ln, :], rstd[:, ln, :], ALU.mult).then_inc(shift_ready[ln], 1)

            def step(s, k):
                if live(s):
                    inverse_std(0, s)
                if live(s - 1):
                    inverse_std(2, s - 1)
                if live(s):
                    inverse_std(1, s)
                if live(s - 3):
                    inverse_std(3, s - 3)
                g = s - 4
                if live(g):
                    for t in range(TILES):
                        pool.wait_ge(weighted_ready, count(g - 1, CHUNKS, 2 * t + 2))
                        first = 2 * t % 4
                        if t >= 2 or live(g - 1):
                            pool.wait_ge(quarter_sum_ready, count(g - 1, TILES, t - 1))
                        halves = half_sum[:, t % 2]
                        pool.tensor_tensor(halves, weighted[:, first], weighted[:, first + 1], ALU.add).then_inc(half_sum_ready, 1)
                        if t == 0:
                            wait_for(pool, y_turned, g - 1)
                        pool.wait_ge(half_sum_ready, count(g - 1, TILES, t + 1))
                        pool.tensor_tensor(quarter_sum[:, t], halves[:, 0:2 * C].rearrange("p (e c) -> p e c", e=2),
                                           halves[:, 2 * C:].rearrange("p (e c) -> p e c", e=2), ALU.add
                                           ).then_inc(quarter_sum_ready, 1)

            run_steps(pool, step)


N_LOADS = 16


def load_count(g, k):
    return (g // 2 + 1) * 16 if isinstance(g, int) else (g - k + 2) * 8


def kernel(**inputs):
    import numpy as np
    import concourse.bacc as bacc
    from concourse.bass_utils import run_bass_kernel_spmd

    p = "L0_conv_"
    arrays = {
        "x": inputs["x"],
        "ln0_g": inputs[p + "ln0_g"], "ln0_b": inputs[p + "ln0_b"],
        "ln1_g": inputs[p + "ln1_g"], "ln1_b": inputs[p + "ln1_b"],
        "ln2_g": inputs[p + "ln2_g"], "ln2_b": inputs[p + "ln2_b"],
        "w_out_t": np.asarray(inputs[p + "W_out"]).T,
        "w_whiten": inputs[p + "W_whiten"],
        "w_key_t": np.asarray(inputs[p + "W_key"]).T,
        "w_recep_t": np.asarray(inputs[p + "W_recep"]).T,
        "w_value_t": np.asarray(inputs[p + "W_value"]).T,
        "router_w": inputs["L0_ffn_router_w"], "router_b": inputs["L0_ffn_router_b"],
        "expert_w": inputs["L0_ffn_expert_w"], "expert_b": inputs["L0_ffn_expert_b"],
        "identity": np.eye(P, dtype=np.float32),
    }
    arrays = {f"in_{n}": np.ascontiguousarray(a) for n, a in arrays.items()}
    nc = bacc.Bacc("TRN2", target_bir_lowering=False, num_devices=1)
    args = [nc.dram_tensor(n, a.shape, mybir.dt.from_np(a.dtype), kind="ExternalInput").ap() for n, a in arrays.items()]
    args.append(nc.dram_tensor("out", arrays["in_x"].shape, F32, kind="ExternalOutput").ap())
    metaformer_layer(nc, *args)
    result = run_bass_kernel_spmd(nc, [arrays], core_ids=[0])
    return result.results[0]["out"]
```

```python
from contextlib import ExitStack

import concourse.bass as bass
from concourse import mybir

P = 128
TILES = 4
TOKENS = TILES * P
SLOTS = 2
UNROLL = 4
ACT = mybir.ActivationFunctionType
ALU = mybir.AluOpType
F32 = mybir.dt.float32
F32R = mybir.dt.float32r
U32 = mybir.dt.uint32

EPS_CHANNEL = 1e-6
EPS = 1e-5
DEPTH = 5
FIRST_LOOPED = 6
X, T0, T1, X1 = range(4)
EARLY, LATE = 0, 1
Y_TURN = 3
Z3_TURN, Z2_TURN = 1, 2
TANH_BLOCK = 1
TILES_IN_STEP = 2


def metaformer_layer(
    nc: bass.Bass,
    x: bass.AP,
    ln0_g: bass.AP,
    ln0_b: bass.AP,
    ln1_g: bass.AP,
    ln1_b: bass.AP,
    ln2_g: bass.AP,
    ln2_b: bass.AP,
    w_out_t: bass.AP,
    w_whiten: bass.AP,
    w_key_t: bass.AP,
    w_recep_t: bass.AP,
    w_value_t: bass.AP,
    router_w: bass.AP,
    router_b: bass.AP,
    expert_w: bass.AP,
    expert_b: bass.AP,
    identity: bass.AP,
    out: bass.AP,
):
    B, C, H, W = x.shape
    HID = w_key_t.shape[1]
    HB = HID // P
    E = router_w.shape[1]
    HALF = E // 2
    PER_IMAGE = H * W // TOKENS
    GROUPS = B * PER_IMAGE
    CHUNKS = 2 * TILES
    assert C == P and H * W % TOKENS == 0 and HALF * P == TOKENS and HB == 4 and E == 8
    ROUNDS = (GROUPS - 2 - FIRST_LOOPED) // UNROLL
    last_looped = FIRST_LOOPED + ROUNDS * UNROLL

    x_groups = x.rearrange("b c h w -> b c (h w)").rearrange("b c (n t) -> c b n t", t=TOKENS)
    out_groups = out.rearrange("b c h w -> b c (h w)").rearrange("b c (n t) -> c b n t", t=TOKENS)

    with ExitStack() as ctx:
        def sb(name, shape, dt=F32):
            return ctx.enter_context(nc.sbuf_tensor(name, shape, dt))

        def sem(name):
            return ctx.enter_context(nc.semaphore(name))

        bank = [ctx.enter_context(nc.psum_tensor(f"bank{i}", [P, TOKENS], F32)) for i in range(8)]
        turn_a, turn_b, value, att = bank[0], bank[1], bank[2], bank[7]
        hidden = [bank[3], bank[4], bank[5], bank[6]]
        expert_ring = [bank[7], bank[2], bank[5], bank[6]]

        def tiled(t):
            return t[:].rearrange("p (t c) -> p t c", t=TILES)

        ident = sb("ident", [P, P])
        over_c = sb("over_c", [P, P])
        less_over_c = sb("less_over_c", [P, P])
        minus_half = sb("minus_half", [P, 3, TILES])
        eps_rows = sb("eps_rows", [P, 4, TILES])
        expert_ids = sb("expert_ids", [P, 2, E])
        g0_row = sb("g0_row", [P, C])
        b0_row = sb("b0_row", [P, C])
        cols = sb("cols", [P, 5])
        g1_col, b1_col, g2_col, b2_col, b2_less_g2 = (cols[:, i:i + 1] for i in range(5))
        wout = sb("wout", [P, C])
        wvalue = sb("wvalue", [P, HB, C])
        mix_hi = sb("mix_hi", [P, HID + C], F32R)
        mix_lo = sb("mix_lo", [P, HID + C], F32R)
        exp_hi = sb("exp_hi", [P, E * C], F32R)
        exp_lo = sb("exp_lo", [P, E * C], F32R)
        rout_parts = sb("rout_parts", [P, 2 * E], F32R)
        whiten = sb("whiten", [P, C])
        keyrecep = sb("keyrecep", [P, HID + C])
        raw_exp = sb("raw_exp", [P, E * C])
        raw_rout = sb("raw_rout", [P, E])
        exp_bias = sb("exp_bias", [1, E * C])
        rout_bias = sb("rout_bias", [1, E])
        merged = sb("merged", [P, HID + C])
        scaled = sb("scaled", [P, HID + C])
        full = sb("full", [P, E * C])
        full_rout = sb("full_rout", [P, E])

        x_in = sb("x_in", [P, SLOTS, TOKENS])
        x_tok = sb("x_tok", [P, SLOTS, TILES, C])
        bn = sb("bn", [P, 4, TILES, 6])
        gap = sb("gap", [P, 4, TILES])
        gap_square = sb("gap_square", [P, 4, TILES])
        both = sb("both", [P, 4, TILES, 2])
        within = sb("within", [P, 4, TILES])
        var_eps = sb("var_eps", [P, 4, TILES])
        neg_mean = sb("neg_mean", [P, 4, TILES])
        rstd = sb("rstd", [P, 4, TILES])
        shift = sb("shift", [P, 4, TILES])
        centred = sb("centred", [P, TILES, C])
        t0 = sb("t0", [P, SLOTS, TILES, C])
        z1 = sb("z1", [P, TILES, C])
        silu = sb("silu", [P, TOKENS])
        t1 = sb("t1", [P, TILES, C])
        carried = sb("carried", [P, SLOTS, TILES, C])
        z2 = sb("z2", [P, TILES, C])
        z2_hi = sb("z2_hi", [P, TOKENS], F32R)
        z2_lo = sb("z2_lo", [P, TOKENS], F32R)
        relu = sb("relu", [P, HB, TOKENS])
        squared = sb("squared", [P, HB, TOKENS])
        gate_tanh = sb("gate_tanh", [P, TILES, C])
        gated_kv = sb("gated_kv", [P, TILES, C])
        x1 = sb("x1", [P, UNROLL, TILES, C])
        z3 = sb("z3", [P, TILES, C])
        z3_hi = sb("z3_hi", [P, TOKENS], F32R)
        z3_lo = sb("z3_lo", [P, TOKENS], F32R)
        cross_logits = sb("cross_logits", [P, TILES, E])
        logits = sb("logits", [P, TILES, E])
        top_logit = sb("top_logit", [P, TILES, 8])
        top_index = sb("top_index", [P, TILES, 8], U32)
        top_id = sb("top_id", [P, TILES, 2])
        logit_gap = sb("logit_gap", [P, TILES])
        gap_tanh = sb("gap_tanh", [P, TILES])
        top_prob = sb("top_prob", [P, TILES, 2])
        one_hot = sb("one_hot", [P, TILES, 2, E])
        gates = sb("gates", [P, TILES, E])
        weighted = sb("weighted", [P, CHUNKS, HALF * C])
        half_sum = sb("half_sum", [P, 2, HALF * C])
        quarter_sum = sb("quarter_sum", [P, 2, 2 * C])
        expert_sum = sb("expert_sum", [P, TILES, C])
        y_out = sb("y_out", [P, SLOTS, TOKENS])

        weights_loaded, prep_pe, prep_dve, prep_pool = (sem(n) for n in ("weights_loaded", "prep_pe", "prep_dve", "prep_pool"))
        x_loaded = [sem(f"x_loaded{i}") for i in range(SLOTS)]
        y_stored = [sem(f"y_stored{i}") for i in range(SLOTS)]
        x_turned, z1_turned, z2_turned, z3_turned = (sem(n) for n in ("x_turned", "z1_turned", "z2_turned", "z3_turned"))
        att_done, recep_done, value_done, router_done, y_turned = (
            sem(n) for n in ("att_done", "recep_done", "value_done", "router_done", "y_turned"))
        key_done = sem("key_done")
        experts_done = sem("experts_done")
        x_tok_ready, z1_ready, silu_ready, z2_ready, z2_hi_ready = (
            sem(n) for n in ("x_tok_ready", "z1_ready", "silu_ready", "z2_ready", "z2_hi_ready"))
        relu_ready, squared_ready = sem("relu_ready"), sem("squared_ready")
        gate_ready, z3_ready, z3_hi_ready, gap_tanh_ready, y_ready = (
            sem(n) for n in ("gate_ready", "z3_ready", "z3_hi_ready", "gap_tanh_ready", "y_ready"))
        bn_ready, both_ready, within_ready, var_eps_ready = (
            [sem(f"{n}_{when}_ready") for when in ("early", "late")] for n in ("bn", "both", "within", "var_eps"))
        centred_ready, t0_ready, t1_ready, z2_lo_ready = (
            sem(n) for n in ("centred_ready", "t0_ready", "t1_ready", "z2_lo_ready"))
        gated_kv_ready, x1_ready, z3_lo_ready = (sem(n) for n in ("gated_kv_ready", "x1_ready", "z3_lo_ready"))
        cross_logits_ready, logits_ready = sem("cross_logits_ready"), sem("logits_ready")
        top_logit_ready, top_index_ready, logit_gap_ready, top_id_ready, top_prob_ready, one_hot_ready, one_hot_weighted, gates_ready = (
            sem(n) for n in ("top_logit_ready", "top_index_ready", "logit_gap_ready", "top_id_ready", "top_prob_ready",
                             "one_hot_ready", "one_hot_weighted", "gates_ready"))
        weighted_ready = sem("weighted_ready")
        rstd_ready, shift_ready = sem("rstd_ready"), sem("shift_ready")
        rstd_x_ready = sem("rstd_x_ready")
        carried_ready = sem("carried_ready")
        half_sum_ready, quarter_sum_ready, expert_sum_ready = (
            sem(n) for n in ("half_sum_ready", "quarter_sum_ready", "expert_sum_ready"))

        def count(g, per=1, extra=0):
            return (g + 1) * per + extra

        def live(g):
            return 0 <= g < GROUPS if isinstance(g, int) else True

        def wait_for(eng, semaphore, g, per=1, extra=0):
            if live(g):
                eng.wait_ge(semaphore, count(g, per, extra))

        def wait_first(eng, *choices):
            for semaphore, g, per, extra in choices:
                if live(g):
                    eng.wait_ge(semaphore, count(g, per, extra))
                    return

        def late_rows(s):
            rows = [row for row, g in ((T0, s), (T1, s - 1), (X1, s - 3)) if live(g)]
            return (rows[0], rows[-1] + 1) if rows else None

        def run_steps(eng, step):
            for s in range(FIRST_LOOPED):
                step(s, s % UNROLL)
            with eng.Fori(0, ROUNDS) as turn:
                for i in range(UNROLL):
                    step(turn * UNROLL + FIRST_LOOPED + i, (FIRST_LOOPED + i) % UNROLL)
            for s in range(last_looped, GROUPS + DEPTH):
                step(s, s % UNROLL)

        block = ctx.enter_context(nc.Block())

        @block.sync
        def _(sp):
            loads = [
                (ident[:], identity), (whiten[:], w_whiten), (keyrecep[:, 0:HID], w_key_t), (keyrecep[:, HID:], w_recep_t),
                (cols[:, 0:1], ln1_g.unsqueeze(1)), (cols[:, 1:2], ln1_b.unsqueeze(1)),
                (cols[:, 2:3], ln2_g.unsqueeze(1)), (cols[:, 3:4], ln2_b.unsqueeze(1)),
                (g0_row[:], ln0_g.unsqueeze(0).to_broadcast([P, C])), (b0_row[:], ln0_b.unsqueeze(0).to_broadcast([P, C])),
                (raw_exp[:].rearrange("p (e c) -> p e c", e=E), expert_w.rearrange("e d c -> d e c")),
                (raw_rout[:], router_w), (exp_bias[:], expert_b.rearrange("e c -> (e c)").unsqueeze(0)),
                (rout_bias[:], router_b.unsqueeze(0)), (wout[:], w_out_t),
                (wvalue[:], w_value_t.rearrange("(j p) c -> p j c", p=P)),
            ]
            assert len(loads) == N_LOADS
            for g in range(2):
                sp.dma_start(x_in[:, g, :], x_groups[:, 0, g, :]).then_inc(x_loaded[g], 16)
            for dst, src in loads:
                sp.dma_start(dst, src).then_inc(weights_loaded, 16)

            def step(s, q):
                k = q % SLOTS
                g = s + 2
                if live(g):
                    wait_for(sp, x_turned, s)
                    sp.dma_start(x_in[:, k, :], x_groups[:, g // PER_IMAGE, g % PER_IMAGE, :]).then_inc(x_loaded[k], 16)
                g = s - 5
                if live(g):
                    wait_for(sp, y_ready, g)
                    sp.dma_start(out_groups[:, g // PER_IMAGE, g % PER_IMAGE, :], y_out[:, 1 - k, :]).then_inc(y_stored[1 - k], 16)

            run_steps(sp, step)
            for k in range(SLOTS):
                sp.wait_ge(y_stored[k], 16 * ((GROUPS + 1 - k) // 2))

        @block.tensor
        def _(pe):
            def split_product(dst, lhs_hi, lhs_lo, rhs_hi, rhs_lo):
                pe.matmul(dst, lhs_hi, rhs_hi, start=True, stop=False)
                pe.matmul(dst, lhs_hi, rhs_lo, start=False, stop=False)
                return pe.matmul(dst, lhs_lo, rhs_hi, start=False, stop=True)

            pe.wait_ge(weights_loaded, 16 * N_LOADS)
            pe.wait_ge(prep_pool, 1)
            pe.matmul(bank[3][:], whiten[:], keyrecep[:, 0:HID], start=True, stop=True)
            pe.matmul(bank[4][:, 0:C], whiten[:], keyrecep[:, HID:], start=True, stop=True).then_inc(prep_pe, 1)
            pe.wait_ge(prep_dve, 3)
            pe.matmul(bank[5][:], over_c[:], scaled[:, 0:HID], start=True, stop=True)
            pe.matmul(bank[6][:, 0:C], over_c[:], scaled[:, HID:], start=True, stop=True).then_inc(prep_pe, 1)
            for h in range(2):
                part = slice(h * TOKENS, (h + 1) * TOKENS)
                pe.matmul(bank[1 + h][:], less_over_c[:], raw_exp[:, part], start=True, stop=False)
                pe.matmul(bank[1 + h][:], over_c[0:1, :], exp_bias[:, part], start=False, stop=True)
            pe.matmul(bank[7][:, 0:E], less_over_c[:], raw_rout[:], start=True, stop=False)
            pe.matmul(bank[7][:, 0:E], over_c[0:1, :], rout_bias[:], start=False, stop=True).then_inc(prep_pe, 1)
            pe.wait_ge(prep_dve, 10)

            def turn(dst, src_tile, done):
                for i in range(TILES):
                    last = pe.transpose(dst[:, i * P:(i + 1) * P], src_tile(i), ident[:])
                last.then_inc(done, 1)

            def step(s, q):
                k = q % SLOTS
                g = s
                if live(g):
                    pe.wait_ge(x_loaded[k], load_count(g, k))
                    wait_first(pe, (y_ready, s - 6, 1, 0), (x_tok_ready, s - 1, 1, 0))
                    turn(turn_b, lambda t: x_in[:, k, t * P:(t + 1) * P], x_turned)
                g = s - 3
                if live(g):
                    wait_for(pe, squared_ready, g, HB)
                    if live(s - 5):
                        pe.wait_ge(weighted_ready, count(s - 6, CHUNKS, 6))
                    else:
                        wait_for(pe, gated_kv_ready, s - 4)
                for t in range(TILES):
                    g = s - 3
                    if live(g):
                        for j in range(HB):
                            last = pe.matmul(value[:, t * C:(t + 1) * C], squared[:, j, t * P:(t + 1) * P], wvalue[:, j, :],
                                             start=(j == 0), stop=(j == HB - 1))
                        if t == TILES - 1:
                            last.then_inc(value_done, 1)
                    g = s - 4
                    if t == Z3_TURN and live(g):
                        wait_for(pe, z3_ready, g)
                        wait_for(pe, relu_ready, s - 3, HB)
                        turn(hidden[0], lambda t: z3[:, t, :], z3_turned)
                    g = s - 2
                    if t == Z2_TURN and live(g):
                        wait_for(pe, z2_ready, g)
                        wait_for(pe, gate_ready, s - 3)
                        turn(turn_a, lambda t: z2[:, t, :], z2_turned)
                g = s - 1
                if live(g):
                    wait_for(pe, z1_ready, g)
                    wait_for(pe, relu_ready, s - 3, HB)
                    turn(hidden[1], lambda t: z1[:, t, :], z1_turned)
                g = s - 4
                if live(g):
                    wait_for(pe, z3_lo_ready, g)
                    wait_first(pe, (weighted_ready, s - 5, CHUNKS, 0), (relu_ready, s - 3, HB, 0))
                    for t in range(TILES):
                        tok, both_parts = slice(t * P, (t + 1) * P), hidden[3][:, t * 2 * E:(t + 1) * 2 * E]
                        pe.matmul(both_parts, z3_hi[:, tok], rout_parts[:], start=True, stop=False)
                        last = pe.matmul(both_parts[:, 0:E], z3_lo[:, tok], rout_parts[:, 0:E], start=False, stop=True)
                    last.then_inc(router_done, 1)
                g = s - 1
                if live(g):
                    wait_for(pe, silu_ready, g)
                    if live(s - 5):
                        pe.wait_ge(weighted_ready, count(s - 6, CHUNKS, 5))
                    else:
                        wait_for(pe, t1_ready, s - 2)
                    for t in range(TILES):
                        last = pe.matmul(att[:, t * C:(t + 1) * C], silu[:, t * P:(t + 1) * P], wout[:], start=True, stop=True)
                    last.then_inc(att_done, 1)
                g = s - 2
                if live(g):
                    wait_for(pe, z2_lo_ready, g)
                    for j in range(HB):
                        if j == 0:
                            wait_first(pe, (z3_lo_ready, s - 4, 1, 0), (relu_ready, s - 3, HB, 0))
                        elif j == 1:
                            wait_first(pe, (silu_ready, s - 1, 1, 0), (relu_ready, s - 3, HB, 0))
                        elif j == 2 and live(s - 5):
                            pe.wait_ge(weighted_ready, count(s - 6, CHUNKS, 7))
                        elif j == 3:
                            wait_first(pe, (logits_ready, s - 4, 1, 0), (relu_ready, s - 3, HB, 0))
                        cut = slice(j * P, (j + 1) * P)
                        split_product(hidden[j][:], mix_hi[:, cut], mix_lo[:, cut], z2_hi[:], z2_lo[:]).then_inc(key_done, 1)
                    for t in range(TILES):
                        tok = slice(t * P, (t + 1) * P)
                        last = split_product(turn_a[:, t * C:(t + 1) * C], z2_hi[:, tok], z2_lo[:, tok], mix_hi[:, HID:], mix_lo[:, HID:])
                    last.then_inc(recep_done, 1)
                for c in range(CHUNKS):
                    g = s - 4
                    if live(g):
                        t, h = divmod(c, 2)
                        if c == 0:
                            wait_first(pe, (t1_ready, s - 1, 1, 0), (weighted_ready, g - 1, CHUNKS, 0))
                        elif c == 1:
                            wait_first(pe, (gated_kv_ready, s - 3, 1, 0), (weighted_ready, g - 1, CHUNKS, 0))
                        elif c < 4:
                            wait_first(pe, (relu_ready, s - 2, HB, c + 1 - HB), (logits_ready, g, 1, 0))
                        else:
                            pe.wait_ge(weighted_ready, count(g - 1, CHUNKS, c - 3))
                        tok, cut = slice(t * P, (t + 1) * P), slice(h * TOKENS, (h + 1) * TOKENS)
                        split_product(expert_ring[c % 4][:], z3_hi[:, tok], z3_lo[:, tok], exp_hi[:, cut], exp_lo[:, cut]
                                      ).then_inc(experts_done, 1)
                    g = s - 5
                    if c == Y_TURN and live(g):
                        wait_for(pe, expert_sum_ready, g, TILES)
                        wait_first(pe, (x_tok_ready, s, 1, 0), (y_ready, s - 6, 1, 0))
                        for t in range(TILES):
                            dst = turn_b[:, t * P:(t + 1) * P]
                            pe.matmul(dst, x1[:, (q - 5) % UNROLL, t, :], ident[:], is_transpose=True, start=True, stop=False)
                            last = pe.matmul(dst, expert_sum[:, t, :], ident[:], is_transpose=True, start=False, stop=True)
                        last.then_inc(y_turned, 1)

            run_steps(pe, step)

        @block.scalar
        def _(act):
            def normalise(dst, src, row, ready):
                for t in range(TILES):
                    last = act.activation(dst[:, t, :], src[:, t, :], ACT.Identity,
                                          bias=shift[:, row, t:t + 1], scale=rstd[:, row, t:t + 1])
                last.then_inc(ready, 1)

            act.wait_ge(weights_loaded, 16 * N_LOADS)

            def step(s, q):
                k = q % SLOTS
                g = s - 4
                if live(g):
                    wait_for(act, z3_turned, g)
                    wait_for(act, experts_done, g - 1, CHUNKS)
                    act.activation(z3_hi[:], hidden[0][:], ACT.Identity, bias=1.0).then_inc(z3_hi_ready, 1)
                g = s - 1
                if live(g):
                    act.wait_ge(shift_ready, count(g))
                    wait_for(act, z1_turned, g - 1)
                    normalise(z1, t0[:, 1 - k], T0, z1_ready)
                g = s - 2
                if live(g):
                    wait_for(act, z2_turned, g)
                    wait_for(act, recep_done, g - 1)
                    act.activation(z2_hi[:], turn_a[:], ACT.Identity, bias=1.0).then_inc(z2_hi_ready, 1)
                g = s - 1
                if live(g):
                    wait_for(act, z1_turned, g)
                    wait_for(act, att_done, g - 1)
                    act.activation(silu[:], hidden[1][:], ACT.Silu, bias=b1_col, scale=g1_col).then_inc(silu_ready, 1)
                for j in range(HB + 1):
                    g = s - 2
                    if live(g):
                        if j < HB:
                            act.wait_ge(key_done, count(g - 1, HB, j + 1))
                            act.activation(relu[:, j, :], hidden[j][:], ACT.Relu).then_inc(relu_ready, 1)
                        if j == 1:
                            wait_for(act, value_done, g - 1)
                        if j > 0:
                            act.wait_ge(relu_ready, count(g - 1, HB, j))
                            act.activation(squared[:, j - 1, :], relu[:, j - 1, :], ACT.Square).then_inc(squared_ready, 1)
                    g = s - 4
                    if j == TANH_BLOCK and live(g):
                        wait_for(act, logit_gap_ready, g)
                        act.activation(gap_tanh[:], logit_gap[:], ACT.Tanh, scale=0.5).then_inc(gap_tanh_ready, 1)
                g = s - 2
                if live(g):
                    wait_for(act, recep_done, g)
                    wait_for(act, gated_kv_ready, g - 1)
                    act.activation(gate_tanh[:], tiled(turn_a), ACT.Tanh, scale=0.5).then_inc(gate_ready, 1)
                g = s - 5
                if live(g):
                    wait_for(act, y_turned, g)
                    if live(g - 2):
                        act.wait_ge(y_stored[1 - k], load_count(g - 2, 1 - k))
                    act.activation(y_out[:, 1 - k, :], turn_b[:], ACT.Copy).then_inc(y_ready, 1)
                g = s - 3
                if live(g):
                    act.wait_ge(shift_ready, count(s))
                    wait_for(act, z3_turned, g - 1)
                    normalise(z3, x1[:, (q - 3) % UNROLL], X1, z3_ready)
                g = s + 1
                if live(g):
                    wait_for(act, x_turned, g)
                    wait_for(act, carried_ready, g - 2)
                    act.activation(x_tok[:, 1 - k, :, :], tiled(turn_b), ACT.Copy).then_inc(x_tok_ready, 1)
                g = s - 1
                if live(g):
                    act.wait_ge(shift_ready, count(s))
                    wait_for(act, z2_turned, g - 1)
                    normalise(z2, t1, T1, z2_ready)
            act.wait_ge(x_turned, 1)
            act.activation(x_tok[:, 0, :, :], tiled(turn_b), ACT.Copy).then_inc(x_tok_ready, 1)
            run_steps(act, step)

        @block.vector
        def _(dve):
            dve.wait_ge(weights_loaded, 16 * N_LOADS)
            dve.tensor_tensor(b2_less_g2, b2_col, g2_col, ALU.subtract).then_inc(prep_dve, 1)
            dve.wait_ge(prep_pe, 1)
            dve.tensor_copy(merged[:, 0:HID], bank[3][:])
            dve.tensor_copy(merged[:, HID:], bank[4][:, 0:C]).then_inc(prep_dve, 1)
            dve.wait_ge(prep_dve, 2)
            dve.tensor_scalar(scaled[:], merged[:], b2_less_g2, None, ALU.mult).then_inc(prep_dve, 1)
            dve.wait_ge(prep_pe, 2)
            dve.scalar_tensor_tensor(full[:, 0:HID], merged[:, 0:HID], g2_col, bank[5][:], ALU.mult, ALU.add)
            dve.scalar_tensor_tensor(full[:, HID:HID + C], merged[:, HID:], g2_col, bank[6][:, 0:C], ALU.mult, ALU.add
                                     ).then_inc(prep_dve, 1)
            dve.wait_ge(prep_dve, 4)
            dve.tensor_copy(mix_hi[:], full[:, 0:HID + C]).then_inc(prep_dve, 1)
            dve.wait_ge(prep_dve, 5)
            dve.tensor_tensor(mix_lo[:], full[:, 0:HID + C], mix_hi[:].bitcast(F32), ALU.subtract).then_inc(prep_dve, 1)
            dve.wait_ge(prep_pe, 3)
            dve.wait_ge(prep_dve, 6)
            for h in range(2):
                part = slice(h * TOKENS, (h + 1) * TOKENS)
                dve.tensor_tensor(full[:, part], bank[1 + h][:], raw_exp[:, part], ALU.add)
            dve.tensor_tensor(full_rout[:], bank[7][:, 0:E], raw_rout[:], ALU.add).then_inc(prep_dve, 1)
            dve.wait_ge(prep_dve, 7)
            dve.tensor_copy(exp_hi[:], full[:])
            dve.tensor_copy(rout_parts[:, 0:E], full_rout[:]).then_inc(prep_dve, 1)
            dve.wait_ge(prep_dve, 8)
            dve.tensor_tensor(exp_lo[:], full[:], exp_hi[:].bitcast(F32), ALU.subtract)
            dve.tensor_tensor(rout_parts[:, E:], full_rout[:], rout_parts[:, 0:E].bitcast(F32), ALU.subtract).then_inc(prep_dve, 1)
            dve.tensor_scalar(g0_row[:], g0_row[:], 2.0 * (1.0 + EPS) ** -0.5, None, ALU.mult)
            dve.tensor_scalar(b0_row[:], b0_row[:], 2.0, None, ALU.mult)
            dve.tensor_scalar(wout[:], wout[:], 2.0, None, ALU.mult).then_inc(prep_dve, 1)
            dve.wait_ge(prep_dve, 10)
            dve.wait_ge(prep_pool, 2)

            def tile_statistics(src, row):
                for t in range(TILES):
                    last = dve.bn_stats(bn[:, row, t, :], src[:, t, :])
                return last

            def statistics_sums(s, when, lo, hi):
                rows = slice(lo, hi)
                dve.wait_ge(bn_ready[when], count(s))
                dve.tensor_tensor(gap[:, rows], bn[:, rows, :, 1], bn[:, rows, :, 4], ALU.subtract)
                dve.tensor_tensor(both[:, rows], bn[:, rows, :, 1:3], bn[:, rows, :, 4:6], ALU.add).then_inc(both_ready[when], 1)

            def statistics_terms(s, when, lo, hi):
                rows = slice(lo, hi)
                dve.wait_ge(both_ready[when], count(s))
                if not isinstance(s, int) or s > 0:
                    dve.wait_ge(rstd_x_ready if when == EARLY else shift_ready, count(s - 1))
                dve.tensor_tensor(gap_square[:, rows], gap[:, rows], gap[:, rows], ALU.mult)
                dve.tensor_scalar(neg_mean[:, rows], both[:, rows, :, 0], -0.5, None, ALU.mult)
                dve.scalar_tensor_tensor(within[:, rows], both[:, rows, :, 1], 1.0 / C, eps_rows[:, rows], ALU.mult, ALU.add
                                         ).then_inc(within_ready[when], 1)

            def statistics_variance(s, when, lo, hi):
                rows = slice(lo, hi)
                dve.wait_ge(within_ready[when], count(s))
                dve.scalar_tensor_tensor(var_eps[:, rows], gap_square[:, rows], 0.25, within[:, rows], ALU.mult, ALU.add
                                         ).then_inc(var_eps_ready[when], 1)

            def step(s, q):
                k = q % SLOTS
                if live(s):
                    wait_for(dve, x_tok_ready, s)
                    tile_statistics(x_tok[:, k], X).then_inc(bn_ready[EARLY], 1)
                    statistics_sums(s, EARLY, X, X + 1)
                    statistics_terms(s, EARLY, X, X + 1)
                    statistics_variance(s, EARLY, X, X + 1)
                    for t in range(TILES):
                        last = dve.scalar_tensor_tensor(centred[:, t, :], x_tok[:, k, t, :], neg_mean[:, X, t:t + 1], g0_row[:],
                                                        ALU.add, ALU.mult)
                    last.then_inc(centred_ready, 1)
                if live(s - 4):
                    wait_for(dve, z3_hi_ready, s - 4)
                    dve.scalar_tensor_tensor(z3_lo[:], hidden[0][:], 1.0, z3_hi[:].bitcast(F32), ALU.add, ALU.subtract
                                             ).then_inc(z3_lo_ready, 1)
                if live(s - 3):
                    wait_for(dve, value_done, s - 3)
                    wait_for(dve, gate_ready, s - 3)
                    dve.scalar_tensor_tensor(gated_kv[:], gate_tanh[:], 1.0, tiled(value), ALU.add, ALU.mult
                                             ).then_inc(gated_kv_ready, 1)
                if live(s - 2):
                    wait_for(dve, z2_hi_ready, s - 2)
                    wait_for(dve, recep_done, s - 3)
                    dve.scalar_tensor_tensor(z2_lo[:], turn_a[:], 1.0, z2_hi[:].bitcast(F32), ALU.add, ALU.subtract
                                             ).then_inc(z2_lo_ready, 1)
                if live(s - 4):
                    parts = hidden[3][:, 0:TILES * 2 * E].rearrange("p (t e) -> p t e", t=TILES)
                    wait_for(dve, router_done, s - 4)
                    dve.tensor_copy(cross_logits[:], parts[:, :, E:]).then_inc(cross_logits_ready, 1)
                if live(s - 3):
                    dve.wait_ge(gated_kv_ready, count(s - 3))
                    wait_for(dve, carried_ready, s - 3)
                    wait_for(dve, y_turned, s - 3 - UNROLL)
                    dve.tensor_tensor(x1[:, (q - 3) % UNROLL], gated_kv[:], carried[:, 1 - k], ALU.add).then_inc(x1_ready, 1)
                if live(s - 4):
                    dve.wait_ge(cross_logits_ready, count(s - 4))
                    dve.tensor_tensor(logits[:], parts[:, :, 0:E], cross_logits[:], ALU.add).then_inc(logits_ready, 1)
                if live(s):
                    dve.wait_ge(centred_ready, count(s))
                    dve.wait_ge(rstd_x_ready, count(s))
                    for t in range(TILES):
                        last = dve.scalar_tensor_tensor(t0[:, k, t, :], centred[:, t, :], rstd[:, X, t:t + 1], b0_row[:],
                                                        ALU.mult, ALU.add)
                    last.then_inc(t0_ready, 1)
                if live(s - 3):
                    dve.wait_ge(x1_ready, count(s - 3))
                    wait_for(dve, logits_ready, s - 4)
                    last_bn = tile_statistics(x1[:, (q - 3) % UNROLL], X1)
                if live(s - 4):
                    if not live(s - 3):
                        wait_for(dve, logits_ready, s - 4)
                    for t in range(TILES):
                        last = dve.max(top_logit[:, t, :], logits[:, t, :])
                    last.then_inc(top_logit_ready, 1)
                if live(s):
                    dve.wait_ge(t0_ready, count(s))
                    last_bn = tile_statistics(t0[:, k], T0)
                if live(s - 4):
                    dve.wait_ge(top_logit_ready, count(s - 4))
                    wait_for(dve, gap_tanh_ready, s - 5)
                    dve.tensor_tensor(logit_gap[:], top_logit[:, :, 1], top_logit[:, :, 0], ALU.subtract).then_inc(logit_gap_ready, 1)
                    for t in range(TILES):
                        last = dve.max_index(top_index[:, t, :], top_logit[:, t, :], logits[:, t, :])
                    last.then_inc(top_index_ready, 1)
                if live(s - 1):
                    wait_for(dve, att_done, s - 1)
                    wait_for(dve, z2_ready, s - 2)
                    wait_for(dve, carried_ready, s - 2)
                    dve.tensor_tensor(t1[:], tiled(att), t0[:, 1 - k], ALU.add).then_inc(t1_ready, 1)
                if live(s - 1):
                    dve.wait_ge(t1_ready, count(s - 1))
                    last_bn = tile_statistics(t1, T1)
                rows = late_rows(s)
                if rows:
                    last_bn.then_inc(bn_ready[LATE], 1)
                if live(s - 4):
                    dve.wait_ge(top_index_ready, count(s - 4))
                    dve.tensor_copy(top_id[:], top_index[:, :, 0:2]).then_inc(top_id_ready, 1)
                    wait_for(dve, gap_tanh_ready, s - 4)
                    dve.tensor_scalar(top_prob[:, :, 0], gap_tanh[:], -0.5, 0.5, ALU.mult, ALU.add)
                    dve.tensor_scalar(top_prob[:, :, 1], gap_tanh[:], 0.5, 0.5, ALU.mult, ALU.add).then_inc(top_prob_ready, 1)
                if rows:
                    statistics_sums(s, LATE, *rows)
                if live(s - 4):
                    dve.wait_ge(top_id_ready, count(s - 4))
                    for j in range(2):
                        last = dve.tensor_tensor(one_hot[:, :, j, :], expert_ids[:, 0:1, :].to_broadcast([P, TILES, E]),
                                                 top_id[:, :, j:j + 1].to_broadcast([P, TILES, E]), ALU.is_equal)
                    last.then_inc(one_hot_ready, 1)
                if rows:
                    statistics_terms(s, LATE, *rows)
                if live(s - 4):
                    dve.wait_ge(top_prob_ready, count(s - 4))
                    dve.wait_ge(one_hot_ready, count(s - 4))
                    dve.tensor_tensor(one_hot[:], one_hot[:], top_prob[:].unsqueeze(3).to_broadcast([P, TILES, 2, E]), ALU.mult
                                      ).then_inc(one_hot_weighted, 1)
                if rows:
                    statistics_variance(s, LATE, *rows)
                if live(s - 4):
                    dve.wait_ge(one_hot_weighted, count(s - 4))
                    dve.tensor_tensor(gates[:], one_hot[:, :, 0, :], one_hot[:, :, 1, :], ALU.add).then_inc(gates_ready, 1)
                g = s - 4
                if live(g):
                    dve.wait_ge(gates_ready, count(g))
                    for c in range(CHUNKS):
                        t, h = divmod(c, 2)
                        if h == 0:
                            wait_for(dve, half_sum_ready, g - 1, TILES, t + 1 - TILES)
                        dve.wait_ge(experts_done, count(g - 1, CHUNKS, c + 1))
                        dve.tensor_tensor(weighted[:, c].rearrange("p (e c) -> p e c", e=HALF), tiled(expert_ring[c % 4]),
                                          gates[:, t, h * HALF:(h + 1) * HALF].unsqueeze(2).to_broadcast([P, HALF, C]), ALU.mult
                                          ).then_inc(weighted_ready, 1)

            run_steps(dve, step)

        @block.gpsimd
        def _(pool):
            pool.memset(over_c[:], 1.0 / C)
            pool.memset(less_over_c[:], -1.0 / C).then_inc(prep_pool, 1)
            for e in range(E):
                pool.memset(expert_ids[:, :, e:e + 1], float(e))
            for row, eps in ((X, EPS * EPS_CHANNEL / (1.0 + EPS)), (T1, 4 * EPS), (T0, 4 * EPS), (X1, EPS)):
                pool.memset(eps_rows[:, row, :], eps)
            pool.memset(minus_half[:], -0.5).then_inc(prep_pool, 1)
            pool.wait_ge(prep_pool, 2)

            def step(s, q):
                k = q % SLOTS
                def expert_tile(g, t):
                    pool.wait_ge(weighted_ready, count(g - 1, CHUNKS, 2 * t + 2))
                    if t >= 2 or live(g - 1):
                        pool.wait_ge(quarter_sum_ready, count(g - 1, TILES, t - 1))
                    halves = half_sum[:, t % 2]
                    pool.tensor_tensor(halves, weighted[:, 2 * t], weighted[:, 2 * t + 1], ALU.add).then_inc(half_sum_ready, 1)
                    if t >= 2 or live(g - 1):
                        pool.wait_ge(expert_sum_ready, count(g - 1, TILES, t - 1))
                    pool.wait_ge(half_sum_ready, count(g - 1, TILES, t + 1))
                    quarters = quarter_sum[:, t % 2]
                    pool.tensor_tensor(quarters, halves[:, 0:2 * C], halves[:, 2 * C:], ALU.add).then_inc(quarter_sum_ready, 1)
                    if t == 0:
                        wait_for(pool, y_turned, g - 1)
                    pool.wait_ge(quarter_sum_ready, count(g - 1, TILES, t + 1))
                    pool.tensor_tensor(expert_sum[:, t], quarters[:, 0:C], quarters[:, C:], ALU.add).then_inc(expert_sum_ready, 1)

                for t in range(TILES_IN_STEP, TILES):
                    if t == TILES - 1 and live(s):
                        pool.wait_ge(var_eps_ready[EARLY], count(s))
                        wait_for(pool, t0_ready, s - 1)
                        pool.tensor_tensor(rstd[:, X], var_eps[:, X], minus_half[:, 0], ALU.pow).then_inc(rstd_x_ready, 1)
                    if live(s - 5):
                        expert_tile(s - 5, t)
                if live(s - 1):
                    wait_for(pool, t1_ready, s - 1)
                    wait_for(pool, x1_ready, s - 3)
                    pool.tensor_tensor(carried[:, 1 - k], t1[:], x_tok[:, 1 - k], ALU.add).then_inc(carried_ready, 1)
                if late_rows(s):
                    lo, hi = late_rows(s)
                    rows = slice(lo, hi)
                    pool.wait_ge(var_eps_ready[LATE], count(s))
                    for semaphore, g in ((z1_ready, s - 1), (z2_ready, s - 2), (z3_ready, s - 4)):
                        wait_for(pool, semaphore, g)
                    pool.tensor_tensor(rstd[:, rows], var_eps[:, rows], minus_half[:, 0:hi - lo], ALU.pow).then_inc(rstd_ready, 1)
                    pool.wait_ge(rstd_ready, count(s))
                    pool.tensor_tensor(shift[:, rows], neg_mean[:, rows], rstd[:, rows], ALU.mult).then_inc(shift_ready, 1)
                if live(s - 4):
                    for t in range(TILES_IN_STEP):
                        expert_tile(s - 4, t)

            run_steps(pool, step)


N_LOADS = 16


def load_count(g, k):
    return (g // 2 + 1) * 16 if isinstance(g, int) else (g - k + 2) * 8


def kernel(**inputs):
    import numpy as np
    import concourse.bacc as bacc
    from concourse.bass_utils import run_bass_kernel_spmd

    p = "L0_conv_"
    arrays = {
        "x": inputs["x"],
        "ln0_g": inputs[p + "ln0_g"], "ln0_b": inputs[p + "ln0_b"],
        "ln1_g": inputs[p + "ln1_g"], "ln1_b": inputs[p + "ln1_b"],
        "ln2_g": inputs[p + "ln2_g"], "ln2_b": inputs[p + "ln2_b"],
        "w_out_t": np.asarray(inputs[p + "W_out"]).T,
        "w_whiten": inputs[p + "W_whiten"],
        "w_key_t": np.asarray(inputs[p + "W_key"]).T,
        "w_recep_t": np.asarray(inputs[p + "W_recep"]).T,
        "w_value_t": np.asarray(inputs[p + "W_value"]).T,
        "router_w": inputs["L0_ffn_router_w"], "router_b": inputs["L0_ffn_router_b"],
        "expert_w": inputs["L0_ffn_expert_w"], "expert_b": inputs["L0_ffn_expert_b"],
        "identity": np.eye(P, dtype=np.float32),
    }
    arrays = {f"in_{n}": np.ascontiguousarray(a) for n, a in arrays.items()}
    nc = bacc.Bacc("TRN2", target_bir_lowering=False, num_devices=1)
    args = [nc.dram_tensor(n, a.shape, mybir.dt.from_np(a.dtype), kind="ExternalInput").ap() for n, a in arrays.items()]
    args.append(nc.dram_tensor("out", arrays["in_x"].shape, F32, kind="ExternalOutput").ap())
    metaformer_layer(nc, *args)
    result = run_bass_kernel_spmd(nc, [arrays], core_ids=[0])
    return result.results[0]["out"]
```

```python
from contextlib import ExitStack

import concourse.bass as bass
from concourse import mybir

P = 128
TILES = 4
TOKENS = TILES * P
SLOTS = 2
UNROLL = 4
ACT = mybir.ActivationFunctionType
ALU = mybir.AluOpType
F32 = mybir.dt.float32
F32R = mybir.dt.float32r
U32 = mybir.dt.uint32

EPS_CHANNEL = 1e-6
EPS = 1e-5
DEPTH = 5
FIRST_LOOPED = 6
X, T0, T1, X1 = range(4)
EARLY, LATE = 0, 1
Y_TURN = 3
GATED_TURN = 0
Z3_TURN, Z2_TURN = 0, 1
TANH_BLOCK = 2
SCALAR_CHUNK = 1
PAIR = 2
PAIRS = TILES // PAIR


def metaformer_layer(
    nc: bass.Bass,
    x: bass.AP,
    ln0_g: bass.AP,
    ln0_b: bass.AP,
    ln1_g: bass.AP,
    ln1_b: bass.AP,
    ln2_g: bass.AP,
    ln2_b: bass.AP,
    w_out_t: bass.AP,
    w_whiten: bass.AP,
    w_key_t: bass.AP,
    w_recep_t: bass.AP,
    w_value_t: bass.AP,
    router_w: bass.AP,
    router_b: bass.AP,
    expert_w: bass.AP,
    expert_b: bass.AP,
    identity: bass.AP,
    out: bass.AP,
):
    B, C, H, W = x.shape
    HID = w_key_t.shape[1]
    HB = HID // P
    E = router_w.shape[1]
    HALF = E // 2
    PER_IMAGE = H * W // TOKENS
    GROUPS = B * PER_IMAGE
    CHUNKS = 2 * TILES
    assert C == P and H * W % TOKENS == 0 and HALF * P == TOKENS and HB == 4 and E == 8
    ROUNDS = (GROUPS - 2 - FIRST_LOOPED) // UNROLL
    last_looped = FIRST_LOOPED + ROUNDS * UNROLL

    x_groups = x.rearrange("b c h w -> b c (h w)").rearrange("b c (n t) -> c b n t", t=TOKENS)
    out_groups = out.rearrange("b c h w -> b c (h w)").rearrange("b c (n t) -> c b n t", t=TOKENS)

    with ExitStack() as ctx:
        def sb(name, shape, dt=F32):
            return ctx.enter_context(nc.sbuf_tensor(name, shape, dt))

        def sem(name):
            return ctx.enter_context(nc.semaphore(name))

        bank = [ctx.enter_context(nc.psum_tensor(f"bank{i}", [P, TOKENS], F32)) for i in range(8)]
        turn_a, turn_b, value, att = bank[0], bank[1], bank[2], bank[7]
        hidden = [bank[3], bank[4], bank[5], bank[6]]
        expert_ring = [bank[2], bank[7], bank[5], bank[6]]

        def tiled(t):
            return t[:].rearrange("p (t c) -> p t c", t=TILES)

        ident = sb("ident", [P, P])
        over_c = sb("over_c", [P, P])
        less_over_c = sb("less_over_c", [P, P])
        minus_half = sb("minus_half", [P, 2, TILES])
        eps_rows = sb("eps_rows", [P, 4, TILES])
        expert_ids = sb("expert_ids", [P, 2, E])
        g0_row = sb("g0_row", [P, C])
        b0_row = sb("b0_row", [P, C])
        cols = sb("cols", [P, 5])
        g1_col, b1_col, g2_col, b2_col, b2_less_g2 = (cols[:, i:i + 1] for i in range(5))
        wout = sb("wout", [P, C])
        wvalue = sb("wvalue", [P, HB, C])
        mix_hi = sb("mix_hi", [P, HID + C], F32R)
        mix_lo = sb("mix_lo", [P, HID + C], F32R)
        exp_hi = sb("exp_hi", [P, E * C], F32R)
        exp_lo = sb("exp_lo", [P, E * C], F32R)
        rout_parts = sb("rout_parts", [P, 2 * E], F32R)
        whiten = sb("whiten", [P, C])
        keyrecep = sb("keyrecep", [P, HID + C])
        raw_exp = sb("raw_exp", [P, E * C])
        raw_rout = sb("raw_rout", [P, E])
        exp_bias = sb("exp_bias", [1, E * C])
        rout_bias = sb("rout_bias", [1, E])
        merged = sb("merged", [P, HID + C])
        scaled = sb("scaled", [P, HID + C])
        full = sb("full", [P, E * C])
        full_rout = sb("full_rout", [P, E])

        x_in = sb("x_in", [P, SLOTS, TOKENS])
        x_tok = sb("x_tok", [P, SLOTS, TILES, C])
        bn = sb("bn", [P, 4, TILES, 6])
        gap = sb("gap", [P, 4, TILES])
        gap_square = sb("gap_square", [P, 4, TILES])
        both = sb("both", [P, 4, TILES, 2])
        within = sb("within", [P, 4, TILES])
        var_eps = sb("var_eps", [P, 4, TILES])
        neg_mean = sb("neg_mean", [P, 4, TILES])
        rstd = sb("rstd", [P, 4, TILES])
        shift = sb("shift", [P, 4, TILES])
        centred = sb("centred", [P, TILES, C])
        t0 = sb("t0", [P, SLOTS, TILES, C])
        z1 = sb("z1", [P, TILES, C])
        silu = sb("silu", [P, TOKENS])
        t1 = sb("t1", [P, TILES, C])
        carried = sb("carried", [P, SLOTS, TILES, C])
        z2 = sb("z2", [P, TILES, C])
        z2_hi = sb("z2_hi", [P, TOKENS], F32R)
        z2_lo = sb("z2_lo", [P, TOKENS], F32R)
        relu = sb("relu", [P, HB, TOKENS])
        squared = sb("squared", [P, HB, TOKENS])
        gate_tanh = sb("gate_tanh", [P, TOKENS])
        gated_kv = sb("gated_kv", [P, TOKENS])
        x1 = sb("x1", [P, UNROLL, TILES, C])
        z3 = sb("z3", [P, TILES, C])
        z3_hi = sb("z3_hi", [P, TOKENS], F32R)
        z3_lo = sb("z3_lo", [P, TOKENS], F32R)
        logit_parts = sb("logit_parts", [P, TILES, 2 * E])
        logits = sb("logits", [P, TILES, E])
        top_logit = sb("top_logit", [P, TILES, 8])
        top_index = sb("top_index", [P, TILES, 8], U32)
        top_id = sb("top_id", [P, TILES, 2])
        logit_gap = sb("logit_gap", [P, TILES])
        gap_tanh = sb("gap_tanh", [P, TILES])
        top_prob = sb("top_prob", [P, TILES, 2])
        one_hot = sb("one_hot", [P, TILES, 2, E])
        gates = sb("gates", [P, TILES, E])
        weighted = sb("weighted", [P, CHUNKS, HALF * C])
        half_sum = sb("half_sum", [P, PAIR, HALF * C])
        quarter_sum = sb("quarter_sum", [P, PAIR, 2 * C])
        expert_sum = sb("expert_sum", [P, TILES, C])
        y_sum = sb("y_sum", [P, TILES, C])
        y_out = sb("y_out", [P, SLOTS, TOKENS])

        ident_loaded, rows_loaded, mix_loaded, experts_loaded = (
            sem(n) for n in ("ident_loaded", "rows_loaded", "mix_loaded", "experts_loaded"))
        fills_ready, constants_ready = sem("fills_ready"), sem("constants_ready")
        merged_done, mix_means_done, expert_means_done = (
            sem(n) for n in ("merged_done", "mix_means_done", "expert_means_done"))
        rows_doubled, b2_less_g2_ready, merged_ready, scaled_ready = (
            sem(n) for n in ("rows_doubled", "b2_less_g2_ready", "merged_ready", "scaled_ready"))
        full_ready, weights_hi_ready, weights_split = (sem(n) for n in ("full_ready", "weights_hi_ready", "weights_split"))
        x_loaded = [sem(f"x_loaded{i}") for i in range(SLOTS)]
        y_stored = [sem(f"y_stored{i}") for i in range(SLOTS)]
        x_turned, z1_turned, z2_turned, z3_turned = (sem(n) for n in ("x_turned", "z1_turned", "z2_turned", "z3_turned"))
        att_done, recep_done, value_done, router_done, y_turned = (
            sem(n) for n in ("att_done", "recep_done", "value_done", "router_done", "y_turned"))
        gated_turned = sem("gated_turned")
        key_done = sem("key_done")
        experts_done = sem("experts_done")
        x_tok_ready, z1_ready, silu_ready, z2_ready, z2_hi_ready = (
            sem(n) for n in ("x_tok_ready", "z1_ready", "silu_ready", "z2_ready", "z2_hi_ready"))
        relu_ready, squared_ready = sem("relu_ready"), sem("squared_ready")
        gate_ready, z3_ready, z3_hi_ready, gap_tanh_ready, y_ready = (
            sem(n) for n in ("gate_ready", "z3_ready", "z3_hi_ready", "gap_tanh_ready", "y_ready"))
        weighted_scalar_ready = sem("weighted_scalar_ready")
        bn_ready, both_ready, within_ready, var_eps_ready = (
            [sem(f"{n}_{when}_ready") for when in ("early", "late")] for n in ("bn", "both", "within", "var_eps"))
        centred_ready, t0_ready, t1_ready, z2_lo_ready = (
            sem(n) for n in ("centred_ready", "t0_ready", "t1_ready", "z2_lo_ready"))
        gated_kv_ready, x1_ready, z3_lo_ready = (sem(n) for n in ("gated_kv_ready", "x1_ready", "z3_lo_ready"))
        logit_parts_ready, logits_ready = sem("logit_parts_ready"), sem("logits_ready")
        top_logit_ready, top_index_ready, logit_gap_ready, top_id_ready, top_prob_ready, one_hot_ready, one_hot_weighted, gates_ready = (
            sem(n) for n in ("top_logit_ready", "top_index_ready", "logit_gap_ready", "top_id_ready", "top_prob_ready",
                             "one_hot_ready", "one_hot_weighted", "gates_ready"))
        weighted_ready = sem("weighted_ready")
        rstd_t_ready, shift_t_ready = sem("rstd_t_ready"), sem("shift_t_ready")
        rstd_x1_ready, shift_x1_ready = sem("rstd_x1_ready"), sem("shift_x1_ready")
        rstd_x_ready = sem("rstd_x_ready")
        carried_ready = sem("carried_ready")
        half_sum_ready, quarter_sum_ready, expert_sum_ready = (
            sem(n) for n in ("half_sum_ready", "quarter_sum_ready", "expert_sum_ready"))
        y_sum_ready = sem("y_sum_ready")

        def count(g, per=1, extra=0):
            return (g + 1) * per + extra

        def live(g):
            return 0 <= g < GROUPS if isinstance(g, int) else True

        def wait_for(eng, semaphore, g, per=1, extra=0):
            if live(g):
                eng.wait_ge(semaphore, count(g, per, extra))

        def wait_first(eng, *choices):
            for semaphore, g, per, extra in choices:
                if live(g):
                    eng.wait_ge(semaphore, count(g, per, extra))
                    return

        def wait_weighted(eng, g, c):
            if c == SCALAR_CHUNK:
                eng.wait_ge(weighted_scalar_ready, count(g))
            else:
                eng.wait_ge(weighted_ready, count(g - 1, CHUNKS - 1, c + (c < SCALAR_CHUNK)))

        def late_rows(s):
            rows = [row for row, g in ((T0, s), (T1, s - 1), (X1, s - 3)) if live(g)]
            return (rows[0], rows[-1] + 1) if rows else None

        def run_steps(eng, step, prepare={}):
            for s in range(FIRST_LOOPED):
                if s in prepare:
                    prepare[s]()
                step(s, s % UNROLL)
            with eng.Fori(0, ROUNDS) as turn:
                for i in range(UNROLL):
                    step(turn * UNROLL + FIRST_LOOPED + i, (FIRST_LOOPED + i) % UNROLL)
            for s in range(last_looped, GROUPS + DEPTH):
                step(s, s % UNROLL)

        block = ctx.enter_context(nc.Block())

        @block.sync
        def _(sp):
            def load(dst, source, loaded):
                sp.dma_start(dst, source).then_inc(loaded, 16)

            load(ident[:], identity, ident_loaded)
            load(x_in[:, 0, :], x_groups[:, 0, 0, :], x_loaded[0])
            load(g0_row[:], ln0_g.unsqueeze(0).to_broadcast([P, C]), rows_loaded)
            load(b0_row[:], ln0_b.unsqueeze(0).to_broadcast([P, C]), rows_loaded)
            load(wout[:], w_out_t, rows_loaded)
            load(x_in[:, 1, :], x_groups[:, 0, 1, :], x_loaded[1])
            for i, column in enumerate((ln1_g, ln1_b, ln2_g, ln2_b)):
                load(cols[:, i:i + 1], column.unsqueeze(1), mix_loaded)
            load(whiten[:], w_whiten, mix_loaded)
            load(keyrecep[:, 0:HID], w_key_t, mix_loaded)
            load(keyrecep[:, HID:], w_recep_t, mix_loaded)
            load(raw_exp[:].rearrange("p (e c) -> p e c", e=E), expert_w.rearrange("e d c -> d e c"), experts_loaded)
            load(raw_rout[:], router_w, experts_loaded)
            load(exp_bias[:], expert_b.rearrange("e c -> (e c)").unsqueeze(0), experts_loaded)
            load(rout_bias[:], router_b.unsqueeze(0), experts_loaded)
            load(wvalue[:], w_value_t.rearrange("(j p) c -> p j c", p=P), experts_loaded)

            def step(s, q):
                k = q % SLOTS
                g = s + 2
                if live(g):
                    wait_for(sp, x_turned, s)
                    sp.dma_start(x_in[:, k, :], x_groups[:, g // PER_IMAGE, g % PER_IMAGE, :]).then_inc(x_loaded[k], 16)
                g = s - 5
                if live(g):
                    wait_for(sp, y_ready, g)
                    sp.dma_start(out_groups[:, g // PER_IMAGE, g % PER_IMAGE, :], y_out[:, 1 - k, :]).then_inc(y_stored[1 - k], 16)

            run_steps(sp, step)
            for k in range(SLOTS):
                sp.wait_ge(y_stored[k], 16 * ((GROUPS + 1 - k) // 2))

        @block.tensor
        def _(pe):
            def split_product(dst, lhs_hi, lhs_lo, rhs_hi, rhs_lo):
                pe.matmul(dst, lhs_hi, rhs_hi, start=True, stop=False)
                pe.matmul(dst, lhs_hi, rhs_lo, start=False, stop=False)
                return pe.matmul(dst, lhs_lo, rhs_hi, start=False, stop=True)

            def prepare_mix():
                pe.wait_ge(mix_loaded, 16 * MIX_LOADS)
                pe.wait_ge(fills_ready, 1)
                pe.matmul(bank[3][:], whiten[:], keyrecep[:, 0:HID], start=True, stop=True)
                pe.matmul(bank[4][:, 0:C], whiten[:], keyrecep[:, HID:], start=True, stop=True).then_inc(merged_done, 1)
                pe.wait_ge(scaled_ready, 1)
                pe.matmul(bank[5][:], over_c[:], scaled[:, 0:HID], start=True, stop=True)
                pe.matmul(bank[0][:, 0:C], over_c[:], scaled[:, HID:], start=True, stop=True).then_inc(mix_means_done, 1)
                pe.wait_ge(weights_split, 1)

            def prepare_experts():
                pe.wait_ge(experts_loaded, 16 * EXPERT_LOADS)
                pe.wait_ge(t1_ready, 3)
                pe.wait_ge(x_tok_ready, 4)
                for h, means in enumerate((bank[2], bank[7])):
                    part = slice(h * TOKENS, (h + 1) * TOKENS)
                    pe.matmul(means[:], less_over_c[:], raw_exp[:, part], start=True, stop=False)
                    pe.matmul(means[:], over_c[0:1, :], exp_bias[:, part], start=False, stop=True)
                pe.matmul(bank[1][:, 0:E], less_over_c[:], raw_rout[:], start=True, stop=False)
                pe.matmul(bank[1][:, 0:E], over_c[0:1, :], rout_bias[:], start=False, stop=True).then_inc(expert_means_done, 1)
                pe.wait_ge(weights_split, 2)

            def turn(dst, src_tile, done):
                for i in range(TILES):
                    last = pe.transpose(dst[:, i * P:(i + 1) * P], src_tile(i), ident[:])
                last.then_inc(done, 1)

            def step(s, q):
                k = q % SLOTS
                g = s
                if live(g):
                    pe.wait_ge(x_loaded[k], load_count(g, k))
                    wait_first(pe, (y_ready, s - 6, 1, 0), (x_tok_ready, s - 1, 1, 0))
                    turn(turn_b, lambda t: x_in[:, k, t * P:(t + 1) * P], x_turned)
                g = s - 3
                if live(g):
                    wait_for(pe, squared_ready, g, HB)
                    if live(s - 5):
                        wait_weighted(pe, s - 5, 4)
                    else:
                        wait_for(pe, gated_kv_ready, s - 4)
                for j in range(HB):
                    g = s - 3
                    if live(g):
                        last = pe.matmul(value[:], wvalue[:, j, :], squared[:, j, :], start=(j == 0), stop=(j == HB - 1))
                        if j == HB - 1:
                            last.then_inc(value_done, 1)
                    g = s - 4
                    if j == Z3_TURN and live(g):
                        wait_for(pe, z3_ready, g)
                        wait_for(pe, relu_ready, s - 3, HB)
                        turn(hidden[0], lambda t: z3[:, t, :], z3_turned)
                    g = s - 2
                    if j == Z2_TURN and live(g):
                        wait_for(pe, z2_ready, g)
                        wait_for(pe, gate_ready, s - 3)
                        turn(turn_a, lambda t: z2[:, t, :], z2_turned)
                g = s - 4
                if live(g):
                    wait_for(pe, z3_lo_ready, g)
                    wait_for(pe, relu_ready, s - 3, HB)
                    for t in range(TILES):
                        tok, both_parts = slice(t * P, (t + 1) * P), hidden[1][:, t * 2 * E:(t + 1) * 2 * E]
                        pe.matmul(both_parts, z3_hi[:, tok], rout_parts[:], start=True, stop=False)
                        last = pe.matmul(both_parts[:, 0:E], z3_lo[:, tok], rout_parts[:, 0:E], start=False, stop=True)
                    last.then_inc(router_done, 1)
                g = s - 1
                if live(g):
                    wait_for(pe, z1_ready, g)
                    wait_first(pe, (weighted_ready, s - 5, CHUNKS - 1, 0), (relu_ready, s - 3, HB, 0))
                    turn(hidden[3], lambda t: z1[:, t, :], z1_turned)
                wait_for(pe, z2_lo_ready, s - 2)
                for j in range(HB):
                    g = s - 2
                    if live(g):
                        if j == 0:
                            wait_first(pe, (z3_lo_ready, s - 4, 1, 0), (relu_ready, s - 3, HB, 0))
                        elif j == 1:
                            wait_first(pe, (logit_parts_ready, s - 4, 1, 0), (relu_ready, s - 3, HB, 0))
                        elif j == 2 and live(s - 5):
                            wait_weighted(pe, s - 5, 6)
                        elif j == 3:
                            wait_first(pe, (silu_ready, s - 1, 1, 0), (relu_ready, s - 3, HB, 0))
                        cut = slice(j * P, (j + 1) * P)
                        split_product(hidden[j][:], mix_hi[:, cut], mix_lo[:, cut], z2_hi[:], z2_lo[:]).then_inc(key_done, 1)
                    g = s - 3
                    if j == GATED_TURN and live(g):
                        wait_for(pe, gated_kv_ready, g)
                        wait_for(pe, z2_lo_ready, s - 2)
                        turn(turn_a, lambda t: gated_kv[:, t * P:(t + 1) * P], gated_turned)
                g = s - 1
                if live(g):
                    wait_for(pe, silu_ready, g)
                    if isinstance(g, int) and g == 0:
                        pe.wait_ge(rows_doubled, 1)
                    if live(s - 5):
                        wait_weighted(pe, s - 5, 5)
                    else:
                        wait_for(pe, t1_ready, s - 2)
                    for t in range(TILES):
                        last = pe.matmul(att[:, t * C:(t + 1) * C], silu[:, t * P:(t + 1) * P], wout[:], start=True, stop=True)
                    last.then_inc(att_done, 1)
                g = s - 2
                if live(g):
                    wait_for(pe, x1_ready, s - 3)
                    split_product(turn_a[:], mix_hi[:, HID:], mix_lo[:, HID:], z2_hi[:], z2_lo[:]).then_inc(recep_done, 1)
                for c in range(CHUNKS):
                    g = s - 4
                    if live(g):
                        t, h = divmod(c, 2)
                        if c == 0:
                            wait_first(pe, (gated_kv_ready, s - 3, 1, 0), (weighted_ready, g - 1, CHUNKS - 1, 0))
                        elif c == 1:
                            wait_first(pe, (t1_ready, s - 1, 1, 0), (weighted_ready, g - 1, CHUNKS - 1, 0))
                        elif c < 4:
                            wait_first(pe, (relu_ready, s - 2, HB, c + 1 - HB), (logits_ready, g, 1, 0))
                        else:
                            wait_weighted(pe, g, c - 4)
                        tok, cut = slice(t * P, (t + 1) * P), slice(h * TOKENS, (h + 1) * TOKENS)
                        split_product(expert_ring[c % 4][:], z3_hi[:, tok], z3_lo[:, tok], exp_hi[:, cut], exp_lo[:, cut]
                                      ).then_inc(experts_done, 1)
                    g = s - 5
                    if c == Y_TURN and live(g):
                        wait_for(pe, y_sum_ready, g)
                        wait_first(pe, (x_tok_ready, s, 1, 0), (y_ready, s - 6, 1, 0))
                        turn(turn_b, lambda t: y_sum[:, t, :], y_turned)

            pe.wait_ge(ident_loaded, 16)
            run_steps(pe, step, {2: prepare_mix, 4: prepare_experts})

        @block.scalar
        def _(act):
            def normalise(dst, src, row, ready, tiles=range(TILES)):
                for t in tiles:
                    last = act.activation(dst[:, t, :], src[:, t, :], ACT.Identity,
                                          bias=shift[:, row, t:t + 1], scale=rstd[:, row, t:t + 1])
                if t == TILES - 1:
                    last.then_inc(ready, 1)

            def step(s, q):
                k = q % SLOTS
                g = s - 4
                if live(g):
                    wait_for(act, z3_turned, g)
                    wait_for(act, experts_done, g - 1, CHUNKS)
                    act.activation(z3_hi[:], hidden[0][:], ACT.Identity, bias=1.0).then_inc(z3_hi_ready, 1)
                g = s - 2
                if live(g):
                    wait_for(act, z2_turned, g)
                    wait_for(act, recep_done, g - 1)
                    act.activation(z2_hi[:], turn_a[:], ACT.Identity, bias=1.0).then_inc(z2_hi_ready, 1)
                g = s - 1
                if live(g):
                    act.wait_ge(shift_t_ready, count(g))
                    wait_for(act, z1_turned, g - 1)
                    normalise(z1, t0[:, 1 - k], T0, z1_ready)
                g = s - 1
                if live(g):
                    wait_for(act, z1_turned, g)
                    wait_for(act, att_done, g - 1)
                    act.activation(silu[:], hidden[3][:], ACT.Silu, bias=b1_col, scale=g1_col).then_inc(silu_ready, 1)
                for j in range(HB + 1):
                    g = s - 2
                    if live(g):
                        if j < HB:
                            act.wait_ge(key_done, count(g - 1, HB, j + 1))
                            act.activation(relu[:, j, :], hidden[j][:], ACT.Relu).then_inc(relu_ready, 1)
                        if j == 1:
                            wait_for(act, value_done, g - 1)
                        if j > 0:
                            act.wait_ge(relu_ready, count(g - 1, HB, j))
                            act.activation(squared[:, j - 1, :], relu[:, j - 1, :], ACT.Square).then_inc(squared_ready, 1)
                    g = s - 4
                    if j == TANH_BLOCK and live(g):
                        wait_for(act, logit_gap_ready, g)
                        act.activation(gap_tanh[:], logit_gap[:], ACT.Tanh, scale=0.5).then_inc(gap_tanh_ready, 1)
                g = s - 2
                if live(g):
                    wait_for(act, recep_done, g)
                    wait_for(act, gated_kv_ready, g - 1)
                    act.activation(gate_tanh[:], turn_a[:], ACT.Tanh, scale=0.5).then_inc(gate_ready, 1)
                g = s - 4
                if live(g):
                    t, h = divmod(SCALAR_CHUNK, 2)
                    wait_for(act, gates_ready, g)
                    wait_for(act, half_sum_ready, g - 1, PAIRS, t // PAIR + 1 - PAIRS)
                    act.wait_ge(experts_done, count(g - 1, CHUNKS, SCALAR_CHUNK + 1))
                    for e in range(HALF):
                        one = slice(e * C, (e + 1) * C)
                        last = act.activation(weighted[:, SCALAR_CHUNK, one], expert_ring[SCALAR_CHUNK % 4][:, one], ACT.Copy,
                                              scale=gates[:, t, h * HALF + e:h * HALF + e + 1])
                    last.then_inc(weighted_scalar_ready, 1)
                g = s - 5
                if live(g):
                    wait_for(act, y_turned, g)
                    if live(g - 2):
                        act.wait_ge(y_stored[1 - k], load_count(g - 2, 1 - k))
                    act.activation(y_out[:, 1 - k, :], turn_b[:], ACT.Copy).then_inc(y_ready, 1)
                g = s - 3
                if live(g):
                    act.wait_ge(shift_x1_ready, count(g))
                    wait_for(act, z3_turned, g - 1)
                    normalise(z3, x1[:, (q - 3) % UNROLL], X1, z3_ready)
                g = s - 1
                if live(g):
                    act.wait_ge(shift_t_ready, count(s))
                    wait_for(act, z2_turned, g - 1)
                    normalise(z2, t1, T1, z2_ready, range(TILES // 2))
                g = s + 1
                if live(g):
                    wait_for(act, x_turned, g)
                    wait_for(act, carried_ready, g - 2)
                    act.activation(x_tok[:, 1 - k, :, :], tiled(turn_b), ACT.Copy).then_inc(x_tok_ready, 1)
                g = s - 1
                if live(g):
                    normalise(z2, t1, T1, z2_ready, range(TILES // 2, TILES))
            act.wait_ge(x_turned, 1)
            act.activation(x_tok[:, 0, :, :], tiled(turn_b), ACT.Copy).then_inc(x_tok_ready, 1)
            act.wait_ge(mix_loaded, 16 * MIX_LOADS)
            run_steps(act, step)

        @block.vector
        def _(dve):
            def prepare_rows():
                dve.wait_ge(rows_loaded, 16 * ROW_LOADS)
                dve.tensor_scalar(g0_row[:], g0_row[:], 2.0 * (1.0 + EPS) ** -0.5, None, ALU.mult)
                dve.tensor_scalar(b0_row[:], b0_row[:], 2.0, None, ALU.mult)
                dve.tensor_scalar(wout[:], wout[:], 2.0, None, ALU.mult).then_inc(rows_doubled, 1)
                dve.wait_ge(rows_doubled, 1)
                dve.wait_ge(constants_ready, 1)

            def prepare_mix():
                dve.wait_ge(mix_loaded, 16 * MIX_LOADS)
                dve.tensor_tensor(b2_less_g2, b2_col, g2_col, ALU.subtract).then_inc(b2_less_g2_ready, 1)
                dve.wait_ge(merged_done, 1)
                dve.tensor_copy(merged[:, 0:HID], bank[3][:])
                dve.tensor_copy(merged[:, HID:], bank[4][:, 0:C]).then_inc(merged_ready, 1)
                dve.wait_ge(b2_less_g2_ready, 1)
                dve.wait_ge(merged_ready, 1)
                dve.tensor_scalar(scaled[:], merged[:], b2_less_g2, None, ALU.mult).then_inc(scaled_ready, 1)
                dve.wait_ge(mix_means_done, 1)
                dve.scalar_tensor_tensor(full[:, 0:HID], merged[:, 0:HID], g2_col, bank[5][:], ALU.mult, ALU.add)
                dve.scalar_tensor_tensor(full[:, HID:HID + C], merged[:, HID:], g2_col, bank[0][:, 0:C], ALU.mult, ALU.add
                                         ).then_inc(full_ready, 1)
                dve.wait_ge(full_ready, 1)
                dve.tensor_copy(mix_hi[:], full[:, 0:HID + C]).then_inc(weights_hi_ready, 1)
                dve.wait_ge(weights_hi_ready, 1)
                dve.tensor_tensor(mix_lo[:], full[:, 0:HID + C], mix_hi[:].bitcast(F32), ALU.subtract).then_inc(weights_split, 1)

            def prepare_experts():
                dve.wait_ge(expert_means_done, 1)
                dve.wait_ge(weights_split, 1)
                for h, means in enumerate((bank[2], bank[7])):
                    part = slice(h * TOKENS, (h + 1) * TOKENS)
                    dve.tensor_tensor(full[:, part], means[:], raw_exp[:, part], ALU.add)
                dve.tensor_tensor(full_rout[:], bank[1][:, 0:E], raw_rout[:], ALU.add).then_inc(full_ready, 1)
                dve.wait_ge(full_ready, 2)
                dve.tensor_copy(exp_hi[:], full[:])
                dve.tensor_copy(rout_parts[:, 0:E], full_rout[:]).then_inc(weights_hi_ready, 1)
                dve.wait_ge(weights_hi_ready, 2)
                dve.tensor_tensor(exp_lo[:], full[:], exp_hi[:].bitcast(F32), ALU.subtract)
                dve.tensor_tensor(rout_parts[:, E:], full_rout[:], rout_parts[:, 0:E].bitcast(F32), ALU.subtract
                                  ).then_inc(weights_split, 1)

            def tile_statistics(src, row):
                for t in range(TILES):
                    last = dve.bn_stats(bn[:, row, t, :], src[:, t, :])
                return last

            def statistics_sums(s, when, lo, hi):
                rows = slice(lo, hi)
                dve.wait_ge(bn_ready[when], count(s))
                dve.tensor_tensor(gap[:, rows], bn[:, rows, :, 1], bn[:, rows, :, 4], ALU.subtract)
                dve.tensor_tensor(both[:, rows], bn[:, rows, :, 1:3], bn[:, rows, :, 4:6], ALU.add).then_inc(both_ready[when], 1)

            def statistics_terms(s, when, lo, hi):
                rows = slice(lo, hi)
                dve.wait_ge(both_ready[when], count(s))
                if when == LATE and not live(s - 1):
                    if live(s - 2):
                        dve.wait_ge(shift_t_ready, count(s - 1))
                    else:
                        wait_for(dve, shift_x1_ready, s - 4)
                dve.tensor_tensor(gap_square[:, rows], gap[:, rows], gap[:, rows], ALU.mult)
                dve.tensor_scalar(neg_mean[:, rows], both[:, rows, :, 0], -0.5, None, ALU.mult)
                dve.scalar_tensor_tensor(within[:, rows], both[:, rows, :, 1], 1.0 / C, eps_rows[:, rows], ALU.mult, ALU.add
                                         ).then_inc(within_ready[when], 1)

            def statistics_variance(s, when, lo, hi):
                rows = slice(lo, hi)
                dve.wait_ge(within_ready[when], count(s))
                dve.scalar_tensor_tensor(var_eps[:, rows], gap_square[:, rows], 0.25, within[:, rows], ALU.mult, ALU.add
                                         ).then_inc(var_eps_ready[when], 1)

            def step(s, q):
                k = q % SLOTS
                if live(s):
                    wait_for(dve, x_tok_ready, s)
                    tile_statistics(x_tok[:, k], X).then_inc(bn_ready[EARLY], 1)
                    statistics_sums(s, EARLY, X, X + 1)
                    statistics_terms(s, EARLY, X, X + 1)
                    statistics_variance(s, EARLY, X, X + 1)
                    for t in range(TILES):
                        last = dve.scalar_tensor_tensor(centred[:, t, :], x_tok[:, k, t, :], neg_mean[:, X, t:t + 1], g0_row[:],
                                                        ALU.add, ALU.mult)
                    last.then_inc(centred_ready, 1)
                if live(s - 4):
                    wait_for(dve, z3_hi_ready, s - 4)
                    dve.scalar_tensor_tensor(z3_lo[:], hidden[0][:], 1.0, z3_hi[:].bitcast(F32), ALU.add, ALU.subtract
                                             ).then_inc(z3_lo_ready, 1)
                if live(s - 2):
                    wait_for(dve, z2_hi_ready, s - 2)
                    dve.scalar_tensor_tensor(z2_lo[:], turn_a[:], 1.0, z2_hi[:].bitcast(F32), ALU.add, ALU.subtract
                                             ).then_inc(z2_lo_ready, 1)
                if live(s - 3):
                    wait_for(dve, value_done, s - 3)
                    if not live(s - 2):
                        wait_for(dve, gate_ready, s - 3)
                    dve.scalar_tensor_tensor(gated_kv[:], gate_tanh[:], 1.0, value[:], ALU.add, ALU.mult
                                             ).then_inc(gated_kv_ready, 1)
                if live(s - 4):
                    parts = hidden[1][:, 0:TILES * 2 * E].rearrange("p (t e) -> p t e", t=TILES)
                    wait_for(dve, router_done, s - 4)
                    dve.tensor_copy(logit_parts[:], parts).then_inc(logit_parts_ready, 1)
                if live(s):
                    dve.wait_ge(centred_ready, count(s))
                    dve.wait_ge(rstd_x_ready, count(s))
                    for t in range(TILES):
                        last = dve.scalar_tensor_tensor(t0[:, k, t, :], centred[:, t, :], rstd[:, X, t:t + 1], b0_row[:],
                                                        ALU.mult, ALU.add)
                    last.then_inc(t0_ready, 1)
                if live(s - 4):
                    dve.wait_ge(logit_parts_ready, count(s - 4))
                    dve.tensor_tensor(logits[:], logit_parts[:, :, 0:E], logit_parts[:, :, E:], ALU.add).then_inc(logits_ready, 1)
                wait_for(dve, logits_ready, s - 4)
                if live(s):
                    dve.wait_ge(t0_ready, count(s))
                    last_bn = tile_statistics(t0[:, k], T0)
                if live(s - 4):
                    for t in range(TILES):
                        last = dve.max(top_logit[:, t, :], logits[:, t, :])
                    last.then_inc(top_logit_ready, 1)
                if live(s - 3):
                    wait_for(dve, gated_turned, s - 3)
                    wait_for(dve, carried_ready, s - 3)
                    dve.tensor_tensor(x1[:, (q - 3) % UNROLL], tiled(turn_a), carried[:, 1 - k], ALU.add).then_inc(x1_ready, 1)
                if live(s - 4):
                    dve.wait_ge(top_logit_ready, count(s - 4))
                    dve.tensor_tensor(logit_gap[:], top_logit[:, :, 1], top_logit[:, :, 0], ALU.subtract).then_inc(logit_gap_ready, 1)
                    for t in range(TILES):
                        last = dve.max_index(top_index[:, t, :], top_logit[:, t, :], logits[:, t, :])
                    last.then_inc(top_index_ready, 1)
                if live(s - 3):
                    dve.wait_ge(x1_ready, count(s - 3))
                    last_bn = tile_statistics(x1[:, (q - 3) % UNROLL], X1)
                if live(s - 4):
                    dve.wait_ge(top_index_ready, count(s - 4))
                    dve.tensor_copy(top_id[:], top_index[:, :, 0:2]).then_inc(top_id_ready, 1)
                if live(s - 1):
                    wait_for(dve, att_done, s - 1)
                    dve.tensor_tensor(t1[:], tiled(att), t0[:, 1 - k], ALU.add).then_inc(t1_ready, 1)
                if live(s - 4):
                    dve.wait_ge(top_id_ready, count(s - 4))
                    for j in range(2):
                        last = dve.tensor_tensor(one_hot[:, :, j, :], expert_ids[:, 0:1, :].to_broadcast([P, TILES, E]),
                                                 top_id[:, :, j:j + 1].to_broadcast([P, TILES, E]), ALU.is_equal)
                    last.then_inc(one_hot_ready, 1)
                    wait_for(dve, gap_tanh_ready, s - 4)
                    dve.tensor_scalar(top_prob[:, :, 0], gap_tanh[:], -0.5, 0.5, ALU.mult, ALU.add)
                    dve.tensor_scalar(top_prob[:, :, 1], gap_tanh[:], 0.5, 0.5, ALU.mult, ALU.add).then_inc(top_prob_ready, 1)
                if live(s - 1):
                    dve.wait_ge(t1_ready, count(s - 1))
                    last_bn = tile_statistics(t1, T1)
                rows = late_rows(s)
                if rows:
                    last_bn.then_inc(bn_ready[LATE], 1)
                if live(s - 4):
                    dve.wait_ge(top_prob_ready, count(s - 4))
                    dve.wait_ge(one_hot_ready, count(s - 4))
                    dve.tensor_tensor(one_hot[:], one_hot[:], top_prob[:].unsqueeze(3).to_broadcast([P, TILES, 2, E]), ALU.mult
                                      ).then_inc(one_hot_weighted, 1)
                if rows:
                    statistics_sums(s, LATE, *rows)
                if live(s - 4):
                    dve.wait_ge(one_hot_weighted, count(s - 4))
                    dve.tensor_tensor(gates[:], one_hot[:, :, 0, :], one_hot[:, :, 1, :], ALU.add).then_inc(gates_ready, 1)
                if rows:
                    statistics_terms(s, LATE, *rows)
                    statistics_variance(s, LATE, *rows)
                g = s - 4
                if live(g):
                    dve.wait_ge(gates_ready, count(g))
                    for c in range(CHUNKS):
                        if c == SCALAR_CHUNK:
                            continue
                        t, h = divmod(c, 2)
                        if c == 2 * PAIR or c == 0 and not live(s):
                            wait_for(dve, half_sum_ready, g - 1, PAIRS, t // PAIR + 1 - PAIRS)
                        dve.wait_ge(experts_done, count(g - 1, CHUNKS, c + 1))
                        dve.tensor_tensor(weighted[:, c].rearrange("p (e c) -> p e c", e=HALF), tiled(expert_ring[c % 4]),
                                          gates[:, t, h * HALF:(h + 1) * HALF].unsqueeze(2).to_broadcast([P, HALF, C]), ALU.mult
                                          ).then_inc(weighted_ready, 1)

            run_steps(dve, step, {0: prepare_rows, 2: prepare_mix, 4: prepare_experts})

        @block.gpsimd
        def _(pool):
            pool.memset(over_c[:], 1.0 / C)
            pool.memset(less_over_c[:], -1.0 / C).then_inc(fills_ready, 1)
            for e in range(E):
                pool.memset(expert_ids[:, :, e:e + 1], float(e))
            for row, eps in ((X, EPS * EPS_CHANNEL / (1.0 + EPS)), (T1, 4 * EPS), (T0, 4 * EPS), (X1, EPS)):
                pool.memset(eps_rows[:, row, :], eps)
            pool.memset(minus_half[:], -0.5).then_inc(constants_ready, 1)
            pool.wait_ge(constants_ready, 1)

            def step(s, q):
                k = q % SLOTS
                def expert_pair(g, p):
                    for c in range(2 * PAIR * p, 2 * PAIR * (p + 1)):
                        wait_weighted(pool, g, c)
                    if p > 0 or live(g - 1):
                        pool.wait_ge(quarter_sum_ready, count(g - 1, PAIRS, p))
                    chunks = weighted[:, 2 * PAIR * p:2 * PAIR * (p + 1)].rearrange("p (t h) c -> p t h c", h=2)
                    pool.tensor_tensor(half_sum[:], chunks[:, :, 0], chunks[:, :, 1], ALU.add).then_inc(half_sum_ready, 1)
                    if p > 0 or live(g - 1):
                        pool.wait_ge(expert_sum_ready, count(g - 1, PAIRS, p))
                    pool.wait_ge(half_sum_ready, count(g - 1, PAIRS, p + 1))
                    pool.tensor_tensor(quarter_sum[:], half_sum[:, :, 0:2 * C], half_sum[:, :, 2 * C:], ALU.add
                                       ).then_inc(quarter_sum_ready, 1)
                    wait_for(pool, y_sum_ready, g - 1)
                    pool.wait_ge(quarter_sum_ready, count(g - 1, PAIRS, p + 1))
                    pool.tensor_tensor(expert_sum[:, PAIR * p:PAIR * (p + 1)], quarter_sum[:, :, 0:C], quarter_sum[:, :, C:], ALU.add
                                       ).then_inc(expert_sum_ready, 1)

                if live(s):
                    pool.wait_ge(var_eps_ready[EARLY], count(s))
                    wait_for(pool, t0_ready, s - 1)
                    pool.tensor_tensor(rstd[:, X], var_eps[:, X], minus_half[:, 0], ALU.pow).then_inc(rstd_x_ready, 1)
                if live(s - 5):
                    expert_pair(s - 5, 1)
                    wait_for(pool, y_turned, s - 6)
                    wait_for(pool, expert_sum_ready, s - 5, PAIRS)
                    pool.tensor_tensor(y_sum[:], expert_sum[:], x1[:, (q - 5) % UNROLL], ALU.add).then_inc(y_sum_ready, 1)
                if live(s - 1):
                    wait_for(pool, t1_ready, s - 1)
                    wait_for(pool, x1_ready, s - 3)
                    pool.tensor_tensor(carried[:, 1 - k], t1[:], x_tok[:, 1 - k], ALU.add).then_inc(carried_ready, 1)
                if late_rows(s):
                    pool.wait_ge(var_eps_ready[LATE], count(s))
                if live(s - 3):
                    wait_for(pool, z3_ready, s - 4)
                    pool.tensor_tensor(rstd[:, X1], var_eps[:, X1], minus_half[:, 0], ALU.pow).then_inc(rstd_x1_ready, 1)
                    wait_for(pool, rstd_x1_ready, s - 3)
                    pool.tensor_tensor(shift[:, X1], neg_mean[:, X1], rstd[:, X1], ALU.mult).then_inc(shift_x1_ready, 1)
                if live(s) or live(s - 1):
                    lo, hi = (T0 if live(s) else T1), (T1 if live(s - 1) else T0) + 1
                    rows = slice(lo, hi)
                    wait_for(pool, z1_ready, s - 1)
                    wait_for(pool, z2_ready, s - 2)
                    pool.tensor_tensor(rstd[:, rows], var_eps[:, rows], minus_half[:, 0:hi - lo], ALU.pow).then_inc(rstd_t_ready, 1)
                    pool.wait_ge(rstd_t_ready, count(s))
                    pool.tensor_tensor(shift[:, rows], neg_mean[:, rows], rstd[:, rows], ALU.mult).then_inc(shift_t_ready, 1)
                if live(s - 4):
                    expert_pair(s - 4, 0)

            run_steps(pool, step)


ROW_LOADS, MIX_LOADS, EXPERT_LOADS = 3, 7, 5


def load_count(g, k):
    return (g // 2 + 1) * 16 if isinstance(g, int) else (g - k + 2) * 8


def kernel(**inputs):
    import numpy as np
    import concourse.bacc as bacc
    from concourse.bass_utils import run_bass_kernel_spmd

    p = "L0_conv_"
    arrays = {
        "x": inputs["x"],
        "ln0_g": inputs[p + "ln0_g"], "ln0_b": inputs[p + "ln0_b"],
        "ln1_g": inputs[p + "ln1_g"], "ln1_b": inputs[p + "ln1_b"],
        "ln2_g": inputs[p + "ln2_g"], "ln2_b": inputs[p + "ln2_b"],
        "w_out_t": np.asarray(inputs[p + "W_out"]).T,
        "w_whiten": inputs[p + "W_whiten"],
        "w_key_t": np.asarray(inputs[p + "W_key"]).T,
        "w_recep_t": np.asarray(inputs[p + "W_recep"]).T,
        "w_value_t": np.asarray(inputs[p + "W_value"]).T,
        "router_w": inputs["L0_ffn_router_w"], "router_b": inputs["L0_ffn_router_b"],
        "expert_w": inputs["L0_ffn_expert_w"], "expert_b": inputs["L0_ffn_expert_b"],
        "identity": np.eye(P, dtype=np.float32),
    }
    arrays = {f"in_{n}": np.ascontiguousarray(a) for n, a in arrays.items()}
    nc = bacc.Bacc("TRN2", target_bir_lowering=False, num_devices=1)
    args = [nc.dram_tensor(n, a.shape, mybir.dt.from_np(a.dtype), kind="ExternalInput").ap() for n, a in arrays.items()]
    args.append(nc.dram_tensor("out", arrays["in_x"].shape, F32, kind="ExternalOutput").ap())
    metaformer_layer(nc, *args)
    result = run_bass_kernel_spmd(nc, [arrays], core_ids=[0])
    return result.results[0]["out"]
```
